# Optimizing a Trainium2 kernel written in Bass

```python
import numpy as np
import jax
import jax.numpy as jnp

def _softmax(x, axis=-1):
    return jax.nn.softmax(x, axis=axis)

def _gelu(x):
    return jax.nn.gelu(x, approximate=True)

def _silu(x):
    return jax.nn.silu(x)

def _sigmoid(x):
    return jax.nn.sigmoid(x)

def _layernorm(x, axis=-1, eps=1e-05):
    m = jnp.mean(x, axis=axis, keepdims=True)
    v = jnp.var(x, axis=axis, keepdims=True)
    return (x - m) / jnp.sqrt(v + eps)

def _scatter_add(tgt, idx, src, axis=0):
    return tgt.at[idx].add(src)

def _segment_sum(src, seg, n):
    return jax.ops.segment_sum(src, seg, n)
kernel_name = 'mk_gnn_ffn_d1_gnn_r8_bf02b3'

def setup_inputs(seed: int=0):
    np.random.seed(seed)
    _w = jnp.asarray

    def _rec_inputs():
        import jax
        import jax.numpy as jnp
        _gk = jax.random.key(seed)
        x = -0.0002117 + 1 * jax.random.normal(jax.random.fold_in(_gk, 1), (12500, 256), jnp.float32)
        src = jax.random.randint(jax.random.fold_in(_gk, 2), (200000,), 0, 12500, jnp.int32)
        dst = jax.random.randint(jax.random.fold_in(_gk, 3), (200000,), 0, 12500, jnp.int32)
        _o = jnp.argsort(dst, stable=True)
        src = src[_o]
        dst = dst[_o]
        edge_weight = jax.random.uniform(jax.random.fold_in(_gk, 12), (200000,), jnp.float32, 0.0, 1)
        return (x, src, dst, edge_weight)
    x, src, dst, edge_weight = _rec_inputs()

    def _L0_gnn_setup():
        import jax, jax.numpy as jnp
        import numpy as np
        N_NODES = 12500
        N_EDGES = 400000
        N_IN = 256
        N_OUT = 256
        key = jax.random.key(seed)
        k1, k2, k3, k4, k5 = jax.random.split(key, 5)
        x = jax.random.normal(k1, (N_NODES, N_IN), dtype=jnp.float32)
        W = jax.random.normal(k2, (N_IN, N_OUT), dtype=jnp.float32) * (1.0 / np.sqrt(N_IN))
        edge_row = jax.random.randint(k3, (N_EDGES,), 0, N_NODES, dtype=jnp.int32)
        edge_col = jax.random.randint(k4, (N_EDGES,), 0, N_NODES, dtype=jnp.int32)
        edge_val = jax.random.uniform(k5, (N_EDGES,), dtype=jnp.float32)
        return {'x': x, 'W': W, 'edge_row': edge_row, 'edge_col': edge_col, 'edge_val': edge_val}
    _L0_gnn_all = _L0_gnn_setup()
    _L0_gnn_in = {k: v for k, v in _L0_gnn_all.items() if k in ('W',)}
    del _L0_gnn_all

    def _L0_ffn_setup():
        import math
        import jax, jax.numpy as jnp
        import numpy as np
        CAPACITY_FACTOR = 1.25
        key = jax.random.key(seed)
        ks = jax.random.split(key, 5)
        B, L, D, F, E = (8, 1024, 256, 1024, 8)
        h = jax.random.normal(ks[0], (B, L, D), dtype=jnp.float32)
        gate_w = jax.random.normal(ks[1], (D, E), dtype=jnp.float32) * 0.02
        gate_b = jnp.zeros((E,), dtype=jnp.float32)
        w1 = jax.random.normal(ks[2], (E, D, F), dtype=jnp.float32) * (1.0 / math.sqrt(D))
        b1 = jnp.zeros((E, F), dtype=jnp.float32)
        w2 = jax.random.normal(ks[3], (E, F, D), dtype=jnp.float32) * (1.0 / math.sqrt(F))
        b2 = jnp.zeros((E, D), dtype=jnp.float32)
        return {'h': h, 'gate_w': gate_w, 'gate_b': gate_b, 'w1': w1, 'b1': b1, 'w2': w2, 'b2': b2}
    _L0_ffn_all = _L0_ffn_setup()
    _L0_ffn_in = {k: v for k, v in _L0_ffn_all.items() if k in ('gate_w', 'gate_b', 'w1', 'b1', 'w2', 'b2')}
    del _L0_ffn_all
    return {'x': x, 'src': src, 'dst': dst, 'edge_weight': edge_weight, 'L0_gnn_W': _L0_gnn_in['W'], 'L0_ffn_gate_w': _L0_ffn_in['gate_w'], 'L0_ffn_gate_b': _L0_ffn_in['gate_b'], 'L0_ffn_w1': _L0_ffn_in['w1'], 'L0_ffn_b1': _L0_ffn_in['b1'], 'L0_ffn_w2': _L0_ffn_in['w2'], 'L0_ffn_b2': _L0_ffn_in['b2']}

def reference(x, src, dst, edge_weight, L0_gnn_W, L0_ffn_gate_w, L0_ffn_gate_b, L0_ffn_w1, L0_ffn_b1, L0_ffn_w2, L0_ffn_b2):
    import jax
    import jax.numpy as jnp

    def _L0_gnn_ref(x, W, edge_row, edge_col, edge_val):
        import jax, jax.numpy as jnp
        import numpy as np
        N_NODES = 12500
        N_EDGES = 400000
        N_IN = 256
        N_OUT = 256
        support = jnp.matmul(x, W)
        msgs = support[edge_col] * edge_val[:, None]
        out = jax.ops.segment_sum(msgs, edge_row, num_segments=N_NODES)
        return out

    def _L0_ffn_ref(h, gate_w, gate_b, w1, b1, w2, b2):
        import math
        import jax, jax.numpy as jnp
        import numpy as np
        CAPACITY_FACTOR = 1.25
        B, L, D = h.shape
        E = gate_w.shape[1]
        T = B * L
        C = max(1, math.ceil(CAPACITY_FACTOR * T / E))
        x = h.reshape(T, D)
        logits = x @ gate_w + gate_b
        probs = jax.nn.softmax(logits, axis=-1)
        idx = jnp.argmax(probs, axis=-1)
        prb = jnp.take_along_axis(probs, idx[:, None], axis=1)[:, 0]
        one_hot = jax.nn.one_hot(idx, E, dtype=jnp.float32)
        pos = (jnp.cumsum(one_hot, axis=0) * one_hot).sum(-1).astype(jnp.int32) - 1
        kept = pos < C
        pos_safe = jnp.where(kept, pos, C)
        buf = jnp.zeros((E, C, D), dtype=h.dtype).at[idx, pos_safe].set(x, mode='drop')
        hmid = jax.nn.relu(jnp.einsum('ecd,edf->ecf', buf, w1) + b1[:, None, :])
        ybuf = jnp.einsum('ecf,efd->ecd', hmid, w2) + b2[:, None, :]
        pos_g = jnp.minimum(pos, C - 1)
        y_tok = ybuf[idx, pos_g] * (prb * kept)[:, None]
        y = y_tok.reshape(B, L, D)
        y = jnp.nan_to_num(y, nan=0.0, posinf=10000.0, neginf=-10000.0)
        return y
    x = x + _L0_gnn_ref(_layernorm(x, axis=-1), L0_gnn_W, src, dst, edge_weight)
    x = x + _L0_ffn_ref(_layernorm(x, axis=-1)[None], L0_ffn_gate_w, L0_ffn_gate_b, L0_ffn_w1, L0_ffn_b1, L0_ffn_w2, L0_ffn_b2)[0]
    return x

_drawn_inputs = setup_inputs


def setup_inputs(seed=0):
    import zlib

    import numpy as np

    out = dict(_drawn_inputs(seed))
    spreads = {'L0_ffn_gate_b': (0.0, 0.1), 'L0_ffn_b1': (0.0, 0.8), 'L0_ffn_b2': (0.0, 0.8)}
    factors = {}
    for name, (base, spread) in spreads.items():
        noise = np.random.default_rng([zlib.crc32(name.encode()), seed]).standard_normal(out[name].shape)
        drawn = base * np.exp(spread * noise) if base else spread * noise
        out[name] = jnp.asarray(drawn.astype(out[name].dtype))
    for name, factor in factors.items():
        out[name] = (out[name] * factor).astype(out[name].dtype)
    return out
```

```python
import concourse.bass as bass
from concourse import mybir
from contextlib import ExitStack


def bass_gnn_then_top1_ffn(
    nc: bass.Bass,
    x: bass.AP,
    src: bass.AP,
    dst: bass.AP,
    edge_weight: bass.AP,
    gnn_w: bass.AP,
    gate_w: bass.AP,
    gate_b: bass.AP,
    w1: bass.AP,
    b1: bass.AP,
    w2: bass.AP,
    b2: bass.AP,
    out: bass.AP,
):
    f32 = mybir.dt.float32
    i32 = mybir.dt.int32
    u32 = mybir.dt.uint32
    ALU = mybir.AluOpType
    ACT = mybir.ActivationFunctionType
    AX = mybir.AxisListType

    P = 128
    N, D = x.shape
    E = src.shape[0]
    NE = gate_w.shape[1]
    F = w1.shape[2]
    KD = D // P
    KF = F // P
    EPS = 1e-5
    FLT_MAX = 3.4028234663852886e38

    BLOCKS = -(-N // P)
    LASTROWS = N - (BLOCKS - 1) * P
    GB = 7
    GROUPS = BLOCKS // GB
    assert GROUPS * GB == BLOCKS and GROUPS % 2 == 0 and GROUPS >= 6

    TILES = -(-E // P)
    TC = -(-(TILES + BLOCKS - 1) // P)
    STEPS = TC * P
    FULLT = E // P
    TAILE = E - FULLT * P
    U = 16
    ITER = STEPS // U
    CHAINS = 4
    assert STEPS % U == 0 and (TC - 1) * P <= FULLT and BLOCKS <= P and TAILE > 0

    DUMP = N
    ACCR = 99
    ACCROWS = P * ACCR
    assert ACCROWS >= max(N + P, BLOCKS * P)

    CAP = max(1, -(-5 * N // (4 * NE)))
    SLOTS = -(-CAP // 512) * 512
    QT = 4
    QUADS = SLOTS // (QT * P)
    XW = D + 4
    RSTD, NMR, PRB, TOK = D, D + 1, D + 2, D + 3
    TRASH = NE * SLOTS
    assert QUADS % 2 == 0 and NE % 2 == 0

    acc = [nc.dram_tensor(f"acc{c}", (ACCROWS, D), f32).ap() for c in range(CHAINS)]
    support_dram = nc.dram_tensor("support_dram", (BLOCKS * P, D), f32).ap()
    buf = nc.dram_tensor("buf", (TRASH, XW), f32).ap()

    ctx = ExitStack()
    with ctx:
        def sb(name, shape, dt=f32):
            return ctx.enter_context(nc.sbuf_tensor(name, shape, dt))

        def sem(name):
            return ctx.enter_context(nc.semaphore(name))

        big = sb("big", [P, BLOCKS * XW])
        work = sb("work", [P, 12288])
        cols = sb("cols", [P, STEPS, 3])
        pre = sb("pre", [P, 5120])

        def view(region, at, *shape):
            size = 1
            for n in shape:
                size *= n
            v = region[:, at:at + size]
            if len(shape) == 2:
                v = v.rearrange("p (a b) -> p a b", a=shape[0])
            if len(shape) == 3:
                v = v.rearrange("p (a b c) -> p a b c", a=shape[0], b=shape[1])
            return v, at + size

        S, _ = view(big, 0, BLOCKS, D)
        xr, _ = view(big, 0, BLOCKS, XW)
        hT, at = view(big, 0, 2 * KF, QT * P)
        fin_rows, at = view(big, at, 2 * QT, XW)
        fxn, at = view(big, at, QT, D)
        fxT, at = view(big, at, 2 * KD, QT * P)
        res, at = view(big, at, 2 * QT, D)
        guard, at = view(big, at, 6, D)
        masks, at = view(big, at, 2, D)
        masks = masks.bitcast(i32)
        assert at <= BLOCKS * XW
        srcR, at = view(work, 0, TC, P)
        dstR, at = view(work, at, TC, P)
        dstS, at = view(work, at, TC, P)
        wR, at = view(work, at, TC, P)
        OH, at = view(work, at, TC, 2 * P)
        btab = work[0:1, at:at + STEPS].bitcast(i32)
        bpack = work[0:1, at + STEPS:at + STEPS + STEPS // 4].bitcast(i32)
        bpart = work[0:1, 0:STEPS // 2].bitcast(i32).rearrange("a (n k) -> a n k", n=2)
        assert at + STEPS + STEPS // 4 <= 12288
        msg, at = view(work, 0, 8, D)
        gsb, at = view(work, at, 4, P)
        ohw, at = view(work, at, 4, P)
        eqs, at = view(work, at, 4, P)
        junk, at = view(work, at, 2, P)
        w1s, at = view(work, 0, 2 * KD, F)
        w2s, at = view(work, at, 2 * KF, D)
        b2s, at = view(work, at, 2, D)
        assert at <= 12288
        xin, at = view(pre, 0, 2 * GB, D)
        xTs, at = view(pre, at, 2 * KD, P)
        rxn, at = view(pre, 0, 2, D)
        rxT, at = view(pre, at, 2 * KD, P)
        assert at <= 5120

        iota_i = sb("iota_i", [P, STEPS])
        ident = sb("ident", [P, P])
        ones = sb("ones", [P, P])
        before = sb("before", [P, P])
        dump_before = sb("dump_before", [P, P])
        dump_col = sb("dump_col", [P, 1])
        trash_col = sb("trash_col", [P, 1])
        tvals = sb("tvals", [P, TC])
        tokp1 = sb("tokp1", [P, BLOCKS])
        valid = sb("valid", [P, BLOCKS])
        zero = sb("zero", [P, 3 * D])
        Ws = sb("Ws", [P, KD, D])
        gws = sb("gws", [P, KD, NE])
        gbs = sb("gbs", [P, NE])
        b1s = sb("b1s", [P, NE, KF])
        scan_keep = sb("scan_keep", [P, NE, GB + 1])
        hi_i = sb("hi_i", [P, 2, TC], i32)
        keys = sb("keys", [P, 3, TC])
        late = sb("late", [P, 2])
        flag_f = sb("flag_f", [P, 1])
        flag_i = sb("flag_i", [P, 1], i32)
        brow = sb("brow", [P, 2, P])
        colring = sb("colring", [P, 2, 8, 3])
        dups = sb("dups", [P, 8])
        idxr = sb("idxr", [P, 8], u32)
        idxd = sb("idxd", [P, 1], u32)
        stats = sb("stats", [P, 2, GB, 6])
        mv = sb("mv", [P, 2, GB, 2])
        ve = sb("ve", [P, 2, GB])
        sd = sb("sd", [P, 2, GB])
        rs = sb("rs", [P, 2, GB])
        lg = sb("lg", [P, 2, GB, NE])
        pr = sb("pr", [P, 2, GB, NE])
        cand = sb("cand", [P, GB, NE])
        small = sb("small", [P, 8, GB])
        ohx = sb("ohx", [P, NE, GB + 1])
        cum = sb("cum", [P, NE, GB + 1])
        pos = sb("pos", [P, GB, NE])
        slots = sb("slots", [P, BLOCKS], u32)
        fidx = sb("fidx", [P, 2, QT], u32)
        fsm = sb("fsm", [P, QT])

        ps = ctx.enter_context(nc.psum_tensor("ps", [P, 8, 512], f32))
        HB = (0, 1, 2, 7)

        s_const = sem("s_const")
        s_edge = [sem(f"s_edge{i}") for i in range(4)]
        s_pad = sem("s_pad")
        s_w = sem("s_w")
        s_gate = sem("s_gate")
        s_xin = [sem(f"s_xin{i}") for i in range(2)]
        s_xtail = sem("s_xtail")
        s_chain = [sem(f"s_chain{c}") for c in range(CHAINS)]
        s_bufz = sem("s_bufz")
        v_step = sem("v_step")
        s_late = sem("s_late")
        s_latesum = sem("s_latesum")
        s_oh = sem("s_oh")
        s_sel = sem("s_sel")
        s_selread = sem("s_selread")
        s_tables = sem("s_tables")
        s_var = sem("s_var")
        s_sd = sem("s_sd")
        s_xn = sem("s_xn")
        s_xt = sem("s_xt")
        s_xts = sem("s_xts")
        s_sp = sem("s_sp")
        s_S = sem("s_S")
        s_col = sem("s_col")
        s_srow = sem("s_srow")
        s_eq = sem("s_eq")
        s_dup = sem("s_dup")
        s_ohw = sem("s_ohw")
        s_idx = sem("s_idx")
        s_g = sem("s_g")
        s_gs = sem("s_gs")
        s_m = sem("s_m")
        s_msg = sem("s_msg")
        s_taken = sem("s_taken")
        a_taken = sem("a_taken")
        u_turn = sem("u_turn")
        u_sup = sem("u_sup")
        u_col = sem("u_col")
        u_rows = sem("u_rows")
        u_srow = sem("u_srow")
        u_dup = sem("u_dup")
        u_idx = sem("u_idx")
        u_m = sem("u_m")
        u_msg = sem("u_msg")
        u_sent = sem("u_sent")
        s_graph = sem("s_graph")
        s_sum = [sem(f"s_sum{i}") for i in range(4)]
        s_xr = sem("s_xr")
        r_var = sem("r_var")
        r_sd = sem("r_sd")
        r_rs = sem("r_rs")
        r_xn = sem("r_xn")
        r_xt = sem("r_xt")
        r_xts = sem("r_xts")
        r_lg = sem("r_lg")
        r_l = sem("r_l")
        r_ex = sem("r_ex")
        r_cum = sem("r_cum")
        r_pos = sem("r_pos")
        r_slot = sem("r_slot")
        s_disp = sem("s_disp")
        s_base = sem("s_base")
        s_routed = sem("s_routed")
        s_ew = [sem(f"s_ew{i}") for i in range(2)]
        s_rows = [sem(f"s_rows{i}") for i in range(2)]
        f_xn = sem("f_xn")
        f_xt = sem("f_xt")
        f_xts = sem("f_xts")
        f_h = sem("f_h")
        f_hs = sem("f_hs")
        f_y = sem("f_y")
        f_yread = sem("f_yread")
        f_res = sem("f_res")
        f_idx = sem("f_idx")
        f_v = sem("f_v")
        s_out = [sem(f"s_out{i}") for i in range(2)]

        block = ctx.enter_context(nc.Block())

        def since(eng, semaphore, count):
            if isinstance(count, int) and count <= 0:
                return
            eng.wait_ge(semaphore, count)

        def turns(eng, n, body):
            body(0)
            with eng.Fori(1, n - 1) as it:
                body(it)
            body(n - 1)

        def edge_rows(a, shift=0):
            n = (TC - 1) * P * P
            return a[0:n].rearrange("(c p e) -> p c e", p=P, e=P)

        x_groups = x[0:(GROUPS - 1) * GB * P, :].rearrange("(g j p) d -> g p j d", j=GB, p=P)
        LASTG = GROUPS - 1

        @block.sync
        def _(sp):
            tabs = [(src, srcR.bitcast(i32)), (dst, dstR.bitcast(i32)), (edge_weight, wR)]
            sp.wait_ge(s_pad, 4)
            tail0 = (TC - 1) * P
            rows = FULLT - tail0
            for i, (a, r) in enumerate(tabs):
                sp.dma_start(r[:, 0:TC - 1, :], edge_rows(a)).then_inc(s_edge[i], 16)
                sp.dma_start(r[0:rows, TC - 1, :],
                             a[tail0 * P:FULLT * P].rearrange("(p e) -> p e", e=P)).then_inc(s_edge[i], 16)
                sp.dma_start(r[rows:rows + 1, TC - 1, 0:TAILE],
                             a[FULLT * P:E].rearrange("(p e) -> p e", p=1)).then_inc(s_edge[i], 16)
            sh = dstS.bitcast(i32)
            sp.dma_start(sh[0:1, 0, 1:P], dst[0:P - 1].rearrange("(p e) -> p e", p=1)).then_inc(s_edge[3], 16)
            sp.dma_start(sh[1:P, 0, :], dst[P - 1:P * P - 1].rearrange("(p e) -> p e", e=P)).then_inc(s_edge[3], 16)
            sp.dma_start(sh[:, 1:TC - 1, :],
                         dst[P * P - 1:(TC - 1) * P * P - 1].rearrange("(c p e) -> p c e", p=P, e=P))\
              .then_inc(s_edge[3], 16)
            sp.dma_start(sh[0:rows, TC - 1, :],
                         dst[tail0 * P - 1:FULLT * P - 1].rearrange("(p e) -> p e", e=P)).then_inc(s_edge[3], 16)
            sp.dma_start(sh[rows:rows + 1, TC - 1, 0:TAILE],
                         dst[FULLT * P - 1:E - 1].rearrange("(p e) -> p e", p=1)).then_inc(s_edge[3], 16)
            sp.dma_start(Ws[:, :, :], gnn_w.rearrange("(k p) n -> p k n", p=P)).then_inc(s_w, 16)

            def load_x(it):
                for h in range(2):
                    last = isinstance(it, int) and 2 * it + h == LASTG
                    since(sp, s_xt, (it * 2 + h - 1) * GB)
                    if not last:
                        sp.dma_start(xin[:, h * GB:(h + 1) * GB, :],
                                     x_groups[bass.ds(it * 2 + h, 1), :, :, :].rearrange("a p j d -> p (a j) d"))\
                          .then_inc(s_xin[h], 16)
                        continue
                    at = LASTG * GB * P
                    sp.dma_start(xin[:, h * GB:(h + 1) * GB - 1, :],
                                 x[at:at + (GB - 1) * P, :].rearrange("(j p) d -> p j d", p=P)).then_inc(s_xin[h], 16)
                    sp.dma_start(xin[0:LASTROWS, (h + 1) * GB - 1, :], x[N - LASTROWS:N, :]).then_inc(s_xtail, 16)
                    sp.dma_start(xin[LASTROWS:P, (h + 1) * GB - 1, :], zero[0:P - LASTROWS, 0:D]).then_inc(s_xtail, 16)

            sp.wait_ge(s_const, 1)
            turns(sp, GROUPS // 2, load_x)
            sp.dma_start(gws[:, :, :], gate_w.rearrange("(k p) n -> p k n", p=P)).then_inc(s_gate, 16)
            sp.dma_start(gbs[:, :], gate_b.rearrange("(a n) -> a n", a=1).to_broadcast([P, NE])).then_inc(s_gate, 16)
            flat = buf.rearrange("r w -> (r w)").rearrange("(p q f) -> p q f", p=P, f=TRASH * XW // P // 65)
            sp.dma_start(flat, zero[:, 0:flat.shape[2]].rearrange("p (a f) -> p a f", a=1)
                         .to_broadcast([P, 65, flat.shape[2]])).then_inc(s_bufz, 16)
            with nc.allow_non_contiguous_dma(reason="expert biases by column, once"):
                sp.dma_start(b1s[:, :, :], b1.rearrange("e (f p) -> p e f", p=P)).then_inc(s_gate, 16)

            sp.wait_ge(s_graph, 1)

            def load_expert(e, h):
                sp.dma_start(w1s[:, h * KD:(h + 1) * KD, :],
                             w1[bass.ds(e, 1), :, :].rearrange("a (k p) f -> p (a k) f", p=P)).then_inc(s_ew[h], 16)
                sp.dma_start(w2s[:, h * KF:(h + 1) * KF, :],
                             w2[bass.ds(e, 1), :, :].rearrange("a (k p) d -> p (a k) d", p=P)).then_inc(s_ew[h], 16)
                sp.dma_start(b2s[:, h, :], b2[bass.ds(e, 1), :].to_broadcast([P, D])).then_inc(s_ew[h], 16)

            load_expert(0, 0)
            load_expert(1, 1)
            sp.wait_ge(s_xr, GROUPS)
            sp.wait_ge(r_slot, GROUPS)
            full = BLOCKS - 1
            sp.dma_start(out[0:full * P, :].rearrange("(j p) d -> p j d", p=P), xr[:, 0:full, 0:D]).then_inc(s_base, 16)
            sp.dma_start(out[full * P:N, :], xr[0:LASTROWS, full, 0:D]).then_inc(s_base, 16)
            sp.wait_ge(s_base, 32)
            sp.wait_ge(s_routed, 1)

            def ffn_loads(pair):
                for q in range(2 * QUADS):
                    n = pair * (2 * QUADS) + q
                    since(sp, f_res, (n - 1) * QT)
                    row = n * (QT * P)
                    sp.dma_start(fin_rows[:, (q % 2) * QT:(q % 2 + 1) * QT, :],
                                 buf[bass.ds(row, QT * P), :].rearrange("(i p) w -> p i w", p=P))\
                      .then_inc(s_rows[q % 2], 16)
                    if q == 0 and not (isinstance(pair, int) and pair == 0):
                        sp.wait_ge(f_res, pair * (2 * QUADS * QT))
                        load_expert(pair * 2 + 1, 1)
                    if q == QUADS and not (isinstance(pair, int) and pair == NE // 2 - 1):
                        sp.wait_ge(f_res, pair * (2 * QUADS * QT) + QUADS * QT)
                        load_expert(pair * 2 + 2, 0)

            turns(sp, NE // 2, ffn_loads)

        @block.gpsimd
        def _(pool):
            pool.memset(zero[:, :], 0.0).then_inc(s_const, 1)
            c = TC - 1
            pool.iota(srcR.bitcast(i32)[:, c, :], pattern=[[1, P]], base=DUMP, channel_multiplier=0).then_inc(s_pad, 1)
            pool.memset(dstR.bitcast(i32)[:, c, :], N - 1).then_inc(s_pad, 1)
            pool.memset(dstS.bitcast(i32)[:, c, :], N - 1).then_inc(s_pad, 1)
            pool.memset(wR[:, c, :], 0.0).then_inc(s_pad, 1)
            pool.memset(dstS.bitcast(i32)[0:1, 0, 0:1], 0).then_inc(s_const, 1)
            pool.memset(ones[:, :], 1.0).then_inc(s_const, 1)
            pool.memset(ident[:, :], 0.0).then_inc(s_const, 1)
            pool.memset(scan_keep[:, :, :], 1.0).then_inc(s_const, 1)
            pool.iota(iota_i[:, :], pattern=[[1, STEPS]], base=0, channel_multiplier=0,
                      allow_small_or_imprecise_dtypes=True).then_inc(s_const, 1)
            pool.iota(tvals[:, :], pattern=[[P, TC]], base=0, channel_multiplier=1,
                      allow_small_or_imprecise_dtypes=True).then_inc(s_const, 1)
            pool.iota(tokp1[:, :], pattern=[[P, BLOCKS]], base=1, channel_multiplier=1,
                      allow_small_or_imprecise_dtypes=True).then_inc(s_const, 1)
            pool.iota(dump_col[:, :], pattern=[[0, 1]], base=DUMP, channel_multiplier=1,
                      allow_small_or_imprecise_dtypes=True).then_inc(s_const, 1)
            pool.iota(trash_col[:, :], pattern=[[0, 1]], base=TRASH, channel_multiplier=1,
                      allow_small_or_imprecise_dtypes=True).then_inc(s_const, 1)
            pool.iota(dump_before[:, :], pattern=[[0, P]], base=DUMP, channel_multiplier=1,
                      allow_small_or_imprecise_dtypes=True).then_inc(s_const, 1)
            pool.wait_ge(s_const, 11)
            pool.affine_select(out=ident[:, :], in_=ident[:, :], compare_op=ALU.not_equal, fill=1.0, base=0,
                               pattern=[[-1, P]], channel_multiplier=1).then_inc(s_const, 1)
            pool.affine_select(out=before[:, :], in_=ones[:, :], compare_op=ALU.is_gt, fill=0.0, base=0,
                               pattern=[[1, P]], channel_multiplier=-1).then_inc(s_const, 1)
            pool.affine_select(out=dump_before[:, :], in_=dump_before[:, :], compare_op=ALU.is_gt, fill=0.0, base=0,
                               pattern=[[-1, P]], channel_multiplier=1).then_inc(s_const, 1)
            pool.memset(scan_keep[:, :, 0:1], 0.0).then_inc(s_const, 1)

            pool.dma_start(acc[0][0:N, :].rearrange("r d -> (r d)").rearrange("(p q f) -> p q f", p=P, q=4),
                           x.rearrange("r d -> (r d)").rearrange("(p q f) -> p q f", p=P, q=4)).then_inc(s_chain[0], 16)
            tail = (ACCROWS - N) * D // P
            pool.dma_start(acc[0][N:ACCROWS, :].rearrange("r d -> (r d)").rearrange("(p f) -> p f", p=P),
                           zero[:, 0:tail]).then_inc(s_chain[0], 16)
            for a in range(1, CHAINS):
                flat = acc[a].rearrange("(p q r) d -> p q (r d)", p=P, r=3)
                for lo, hi in ((0, 16), (16, ACCR // 3)):
                    pool.dma_start(flat[:, lo:hi, :], zero[:, :].rearrange("p (a f) -> p a f", a=1)
                                   .to_broadcast([P, hi - lo, 3 * D])).then_inc(s_chain[a], 16)

            def add_rows(a, col, rows, done):
                pool.sem_inc(s_taken, 1)
                pool.indirect_dma_start(out=acc[a], out_offset=bass.IndirectOffsetOnAxis(ap=col, axis=0),
                                        in_=rows, in_offset=None, compute_op=ALU.add).then_inc(done, 16)

            pool.wait_ge(s_tables, 1)
            is_sorted = pool.value_load(flag_i[0:1, 0:1], min_val=0, max_val=1)
            with pool.If(is_sorted > 0):
                def scatter(it):
                    for k in range(U):
                        s = it * U + k
                        pool.wait_ge(s_msg, s + 1)
                        pool.wait_ge(s_idx, s + 1)
                        pool.wait_ge(s_chain[k % CHAINS], (it * (U // CHAINS) + k // CHAINS + 2) * 16)
                        add_rows(k % CHAINS, idxr[:, k % 8:k % 8 + 1], msg[:, k % 8, :], s_chain[k % CHAINS])
                turns(pool, ITER, scatter)
                for a in range(CHAINS):
                    pool.wait_ge(s_chain[a], 16 * (2 + STEPS // CHAINS))
                pool.nop().then_inc(s_graph, 1)
            with pool.Else():
                pool.wait_ge(s_S, BLOCKS)
                for a in range(CHAINS):
                    pool.wait_ge(s_chain[a], 32)
                pool.dma_start(support_dram.rearrange("(j p) d -> p j d", p=P), S[:, :, :]).then_inc(u_sup, 16)
                pool.wait_ge(u_sup, 16)
                pool.nop().then_inc(u_turn, 1)
                with pool.Fori(0, STEPS) as s:
                    pool.wait_ge(u_col, s + 1)
                    pool.sem_inc(s_taken, 1)
                    pool.indirect_dma_start(out=msg[:, 1, :], out_offset=None, in_=support_dram,
                                            in_offset=bass.IndirectOffsetOnAxis(ap=idxd[:, 0:1], axis=0))\
                        .then_inc(u_rows, 16)
                    pool.wait_ge(u_msg, s + 1)
                    add_rows(0, idxr[:, 0:1], msg[:, 0, :], u_sent)
                    pool.wait_ge(u_sent, s * 16 + 16)
                    pool.sem_inc(u_turn, 1)
                pool.nop().then_inc(s_graph, 1)

            for w in range(GROUPS + 6):
                for stage in range(CHAINS, -1, -1):
                    q = w - stage
                    if not 0 <= q < GROUPS:
                        continue
                    done = 16 * (CHAINS * (q // 4) + stage)
                    if stage:
                        pool.wait_ge(s_sum[q % 4], done)
                    if stage == CHAINS:
                        pool.nop().then_inc(s_xr, 1)
                        continue
                    rows = acc[stage][q * GB * P:(q + 1) * GB * P, :].rearrange("(j p) d -> p j d", p=P)
                    to = xr[:, q * GB:(q + 1) * GB, 0:D]
                    if stage == 0:
                        pool.dma_start(to, rows).then_inc(s_sum[q % 4], 16)
                    else:
                        pool.dma_start(to, rows, accum_op=ALU.add).then_inc(s_sum[q % 4], 16)
                q = w - 6
                if q < 0:
                    continue
                if q == 0:
                    pool.wait_ge(s_bufz, 16)
                pool.wait_ge(r_slot, q + 1)
                for j in range(q * GB, (q + 1) * GB):
                    pool.indirect_dma_start(out=buf, out_offset=bass.IndirectOffsetOnAxis(ap=slots[:, j:j + 1], axis=0),
                                            in_=xr[:, j, :], in_offset=None, bounds_check=TRASH - 1,
                                            oob_is_err=False).then_inc(s_disp, 16)
            pool.wait_ge(s_disp, 16 * BLOCKS)
            pool.wait_ge(s_base, 32)
            pool.nop().then_inc(s_routed, 1)

            def send(pair):
                for q in range(2 * QUADS):
                    n = pair * (2 * QUADS) + q
                    for i in range(QT):
                        pool.wait_ge(f_res, n * QT + i + 1)
                        pool.sem_inc(s_taken, 1)
                        pool.indirect_dma_start(out=out, out_offset=bass.IndirectOffsetOnAxis(ap=fidx[:, q % 2, i:i + 1], axis=0),
                                                in_=res[:, (q % 2) * QT + i, :], in_offset=None,
                                                bounds_check=N - 1, oob_is_err=False).then_inc(s_out[q % 2], 16)
            turns(pool, NE // 2, send)
            for h in range(2):
                pool.wait_ge(s_out[h], 16 * NE * QUADS * QT // 2)

        @block.vector
        def _(dve):
            chain = [0]

            def link(ins):
                chain[0] += 1
                ins.then_inc(v_step, 1)
                dve.wait_ge(v_step, chain[0])

            srcI, dstI, dstSI = (a.bitcast(i32) for a in (srcR, dstR, dstS))
            dve.wait_ge(s_const, 15)
            for i in range(3):
                dve.wait_ge(s_edge[i], 48)
            dve.wait_ge(s_edge[3], 80)
            nc.vector.tensor_scalar(hi_i[:, 0, :], dstI[:, :, P - 1], 7, None, ALU.arith_shift_right)
            link(nc.vector.tensor_scalar(hi_i[:, 1, :], dstSI[:, :, 0], 7, None, ALU.arith_shift_right))
            nc.vector.tensor_copy(keys[:, 0:2, :], hi_i[:, :, :])
            nc.vector.tensor_copy(srcR[:, :, :], srcI[:, :, :])
            nc.vector.tensor_copy(dstR[:, :, :], dstI[:, :, :])
            link(nc.vector.tensor_copy(dstS[:, :, :], dstSI[:, :, :]))
            nc.vector.tensor_scalar(valid[:, :], tokp1[:, :], float(N), None, ALU.is_le)
            link(nc.vector.tensor_tensor(OH[:, :, 0:P], dstS[:, :, :], dstR[:, :, :], ALU.is_gt))
            nc.vector.tensor_reduce(late[:, 0:1], OH[:, :, 0:P], AX.XY, ALU.add).then_inc(s_late, 1)
            dve.wait_ge(s_latesum, 1)
            link(nc.vector.tensor_scalar(flag_f[:, :], ps[:, 0, 0:1], 0.0, None, ALU.is_equal))
            nc.vector.tensor_copy(flag_i[:, :], flag_f[:, :])
            nc.vector.scalar_tensor_tensor(keys[:, 2, :], keys[:, 0, :], flag_f[:, 0:1], tvals[:, :], ALU.mult, ALU.add)
            link(nc.vector.scalar_tensor_tensor(keys[:, 1, :], keys[:, 1, :], flag_f[:, 0:1], tvals[:, :],
                                                ALU.mult, ALU.add))
            link(nc.vector.tensor_scalar(keys[:, 1, :], keys[:, 1, :], 1.0, None, ALU.subtract))
            for c in range(TC):
                n = 2 * P if c < TC - 1 else P
                link(nc.vector.tensor_scalar(OH[:, c, 0:n], iota_i[:, c * P:c * P + n], keys[:, 1, c:c + 1], None, ALU.is_gt))
                nc.vector.scalar_tensor_tensor(OH[:, c, 0:n], iota_i[:, c * P:c * P + n], keys[:, 2, c:c + 1],
                                               OH[:, c, 0:n], ALU.is_le, ALU.mult).then_inc(s_oh, 1)
            for c in range(TC):
                dve.wait_ge(s_sel, c + 1)
                bank = ps[:, 1 + c % 2, :]
                i0 = c * P
                nc.vector.tensor_copy(cols[:, i0:i0 + P, 0], bank[:, 0:P])
                nc.vector.tensor_copy(cols[:, i0:i0 + P, 2], bank[:, 2 * P:3 * P])
                link(nc.vector.scalar_tensor_tensor(brow[:, c % 2, :], bank[:, 3 * P:4 * P], -1.0, iota_i[:, i0:i0 + P],
                                                    ALU.mult, ALU.add))
                nc.vector.tensor_copy(btab[0:1, i0:i0 + P], brow[0:1, c % 2, :])
                nc.vector.scalar_tensor_tensor(cols[:, i0:i0 + P, 1], brow[:, c % 2, :], float(-P), bank[:, P:2 * P],
                                               ALU.mult, ALU.add).then_inc(s_selread, 1)
            dve.wait_ge(s_selread, TC)
            quad = btab[0:1, :].rearrange("a (n k) -> a n k", k=4)
            link(nc.vector.tensor_copy(bpack[0:1, :], quad[:, :, 0]))
            for k in range(1, 4):
                link(nc.vector.tensor_scalar(bpart[0:1, k % 2, :], quad[:, :, k], 7 * k, None, ALU.logical_shift_left))
                link(nc.vector.tensor_tensor(bpack[0:1, :], bpack[0:1, :], bpart[0:1, k % 2, :], ALU.bitwise_or))
            nc.vector.memset(ohx[:, :, 0:1], 0.0).then_inc(s_tables, 1)

            def norm_stats(rows, h, var_ready):
                for j in range(GB):
                    nc.vector.bn_stats(stats[:, h, j, :], rows(j))
                dve.drain()
                for j in range(GB):
                    nc.vector.bn_aggr(mv[:, h, j, :], stats[:, h, j, :])
                dve.drain()
                nc.vector.tensor_scalar(ve[:, h, :], mv[:, h, :, 1], EPS, None, ALU.add).then_inc(var_ready, 1)

            def norm_x(it):
                for h in range(2):
                    dve.wait_ge(s_xin[h], it * 16 + 16)
                    if isinstance(it, int) and 2 * it + h == LASTG:
                        dve.wait_ge(s_xtail, 32)
                    norm_stats(lambda j: xin[:, h * GB + j, :], h, s_var)
                    dve.wait_ge(s_sd, it * 2 + h + 1)
                    nc.vector.reciprocal(rs[:, h, :], sd[:, h, :])
                    dve.drain()
                    for j in range(GB):
                        nc.vector.tensor_scalar(xin[:, h * GB + j, :], xin[:, h * GB + j, :], mv[:, h, j, 0:1],
                                                rs[:, h, j:j + 1], ALU.subtract, ALU.mult).then_inc(s_xn, 1)
            turns(dve, GROUPS // 2, norm_x)

            is_sorted = dve.value_load(flag_i[0:1, 0:1], min_val=0, max_val=1)
            with dve.If(is_sorted > 0):
                dve.wait_ge(s_S, BLOCKS)

                def take_cols(half, n):
                    nc.vector.tensor_copy(colring[:, half, :, :], cols[:, bass.ds(n * 8, 8), :]).then_inc(s_col, 1)

                take_cols(0, 0)

                def edges(it):
                    last = isinstance(it, int) and it == ITER - 1
                    for k in range(U):
                        s = it * U + k
                        half, c = k // 8, k % 8
                        if k == 4:
                            take_cols(1, it * 2 + 1)
                        if k == 12 and not last:
                            take_cols(0, it * 2 + 2)
                        if c == 0:
                            dve.wait_ge(s_col, it * 2 + half + 1)
                        src_c, dst_c, w_c = (colring[:, half, c, n:n + 1] for n in range(3))
                        dve.wait_ge(s_srow, s + 1)
                        row = ps[:, k % 4, 0:P]
                        nc.vector.scalar_tensor_tensor(junk[:, k % 2, :], row, src_c, dump_before[:, :],
                                                       ALU.is_equal, ALU.mult, accum_out=dups[:, c:c + 1])\
                            .then_inc(s_dup, 1)
                        since(dve, s_g, s - 3)
                        nc.vector.tensor_scalar(eqs[:, k % 4, :], row, src_c, None, ALU.is_equal).then_inc(s_eq, 1)
                        nc.vector.tensor_scalar(ohw[:, k % 4, :], iota_i[:, 0:P], dst_c, w_c, ALU.is_equal, ALU.mult)\
                            .then_inc(s_ohw, 1)
                        if not isinstance(s, int) or s >= 8:
                            dve.wait_ge(s_chain[k % CHAINS], (it * (U // CHAINS) + k // CHAINS + 1) * 16)
                        dve.wait_ge(s_dup, s + 1)
                        nc.vector.tensor_scalar(idxr[:, c:c + 1], dups[:, c:c + 1], src_c, dump_col[:, 0:1],
                                                ALU.max, ALU.min).then_inc(s_idx, 1)
                turns(dve, ITER, edges)
            with dve.Else():
                dve.wait_ge(s_S, BLOCKS)
                with dve.Fori(0, STEPS) as s:
                    dve.wait_ge(u_turn, s + 1)
                    nc.vector.tensor_copy(idxd[:, 0:1], cols[:, bass.ds(s, 1), 1])
                    nc.vector.tensor_copy(colring[:, 0, 0:1, :], cols[:, bass.ds(s, 1), :]).then_inc(u_col, 1)
                    dve.wait_ge(u_srow, s + 1)
                    nc.vector.scalar_tensor_tensor(junk[:, 0, :], ps[:, 0, 0:P], colring[:, 0, 0, 0:1], dump_before[:, :],
                                                   ALU.is_equal, ALU.mult, accum_out=dups[:, 0:1]).then_inc(u_dup, 1)
                    nc.vector.tensor_scalar(eqs[:, 0, :], ps[:, 0, 0:P], colring[:, 0, 0, 0:1], colring[:, 0, 0, 2:3],
                                            ALU.is_equal, ALU.mult)
                    dve.wait_ge(u_dup, s + 1)
                    nc.vector.tensor_scalar(idxr[:, 0:1], dups[:, 0:1], colring[:, 0, 0, 0:1], dump_col[:, 0:1],
                                            ALU.max, ALU.min).then_inc(u_idx, 1)
                dve.nop()

            dve.wait_ge(s_graph, 1)
            dve.wait_ge(s_gate, 48)

            def route(it):
                for h in range(2):
                    q = it * 2 + h
                    dve.wait_ge(s_xr, q + 1)
                    norm_stats(lambda j: xr[:, bass.ds(q * GB + j, 1), 0:D].rearrange("p a d -> p (a d)"), h, r_var)
                    dve.wait_ge(r_sd, q + 1)
                    group = lambda c: xr[:, bass.ds(q * GB, GB), c]
                    nc.vector.reciprocal(rs[:, h, :], sd[:, h, :])
                    dve.drain()
                    nc.vector.tensor_copy(group(RSTD), rs[:, h, :])
                    nc.vector.scalar_tensor_tensor(small[:, 0, :], mv[:, h, :, 0], -1.0, rs[:, h, :], ALU.mult, ALU.mult)
                    dve.drain()
                    nc.vector.tensor_copy(group(NMR), small[:, 0, :])
                    nc.vector.tensor_copy(group(TOK), tokp1[:, bass.ds(q * GB, GB)]).then_inc(r_rs, 1)
                    wide = lambda a: a.rearrange("p (j a) -> p j a", a=1).to_broadcast([P, GB, NE])
                    over_j = lambda a: a.rearrange("p (a e) -> p a e", a=1).to_broadcast([P, GB, NE])
                    dve.wait_ge(r_lg, (q + 1) * GB)
                    logit = ps[:, 4, 0:GB * NE].rearrange("p (j e) -> p j e", e=NE)
                    nc.vector.tensor_tensor(lg[:, h, :, :], logit, over_j(gbs[:, :]), ALU.add)
                    dve.drain()
                    nc.vector.tensor_reduce(small[:, 1, :], lg[:, h, :, :], AX.X, ALU.max)
                    dve.drain()
                    nc.vector.tensor_tensor(lg[:, h, :, :], lg[:, h, :, :], wide(small[:, 1, :]), ALU.subtract)\
                        .then_inc(r_l, 1)
                    dve.wait_ge(r_ex, q + 1)
                    nc.vector.tensor_reduce(small[:, 2, :], lg[:, h, :, :], AX.X, ALU.add)
                    dve.drain()
                    nc.vector.reciprocal(small[:, 3, :], small[:, 2, :])
                    dve.drain()
                    nc.vector.tensor_tensor(pr[:, h, :, :], lg[:, h, :, :], wide(small[:, 3, :]), ALU.mult)
                    dve.drain()
                    nc.vector.tensor_reduce(small[:, 4, :], pr[:, h, :, :], AX.X, ALU.max)
                    dve.drain()
                    nc.vector.tensor_copy(group(PRB), small[:, 4, :])
                    nc.vector.tensor_tensor(cand[:, :, :], pr[:, h, :, :], wide(small[:, 4, :]), ALU.is_equal)
                    dve.drain()
                    nc.vector.scalar_tensor_tensor(cand[:, :, :], cand[:, :, :], float(-NE), over_j(iota_i[:, 0:NE]),
                                                   ALU.mult, ALU.add)
                    dve.drain()
                    nc.vector.tensor_reduce(small[:, 5, :], cand[:, :, :], AX.X, ALU.min)
                    dve.drain()
                    nc.vector.tensor_tensor(cand[:, :, :], cand[:, :, :], wide(small[:, 5, :]), ALU.is_equal)
                    dve.drain()
                    chosen = ohx[:, :, 1:GB + 1].rearrange("p e j -> p j e")
                    nc.vector.tensor_tensor(chosen, cand[:, :, :], wide(valid[:, bass.ds(q * GB, GB)]), ALU.mult)
                    dve.drain()
                    nc.vector.tensor_tensor_scan(cum[:, :, :].rearrange("p e j -> p (e j)"),
                                                 scan_keep[:, :, :].rearrange("p e j -> p (e j)"),
                                                 ohx[:, :, :].rearrange("p e j -> p (e j)"), 0.0, ALU.mult, ALU.add)\
                        .then_inc(r_cum, 1)
                    dve.wait_ge(r_pos, q + 1)
                    count = ps[:, 5, 0:NE * GB].rearrange("p (e j) -> p j e", e=NE)
                    nc.vector.tensor_tensor(pos[:, :, :], count, chosen, ALU.mult)
                    nc.vector.tensor_scalar(small[:, 5, :], small[:, 5, :], float(NE), float(SLOTS), ALU.add, ALU.mult)
                    dve.drain()
                    nc.vector.tensor_reduce(small[:, 6, :], pos[:, :, :], AX.X, ALU.add)
                    nc.vector.tensor_copy(ohx[:, :, 0:1], cum[:, :, GB:GB + 1])
                    dve.drain()
                    nc.vector.scalar_tensor_tensor(small[:, 7, :], small[:, 6, :], float(CAP), valid[:, bass.ds(q * GB, GB)],
                                                   ALU.is_lt, ALU.mult)
                    nc.vector.scalar_tensor_tensor(small[:, 6, :], small[:, 6, :], trash_col[:, 0:1], small[:, 5, :],
                                                   ALU.subtract, ALU.add)
                    dve.drain()
                    nc.vector.tensor_tensor(small[:, 6, :], small[:, 6, :], small[:, 7, :], ALU.mult)
                    dve.drain()
                    nc.vector.tensor_scalar(slots[:, bass.ds(q * GB, GB)], small[:, 6, :], trash_col[:, 0:1], None, ALU.add)\
                        .then_inc(r_slot, 1)
            turns(dve, GROUPS // 2, route)

            dve.wait_ge(s_routed, 1)

            def take_xT(n, h):
                dve.wait_ge(f_xt, n + 1)
                nc.vector.tensor_copy(fxT[:, h * KD:(h + 1) * KD, :], ps[:, 3:3 + KD, :]).then_inc(f_xts, 1)

            take_xT(0, 0)

            def finish(pair):
                last = isinstance(pair, int) and pair == NE // 2 - 1
                for q in range(2 * QUADS):
                    n = pair * (2 * QUADS) + q
                    h = q % 2
                    if not (last and q == 2 * QUADS - 1):
                        take_xT(n + 1, 1 - h)
                    since(dve, s_out[h], (pair * QUADS + q // 2) * (16 * QT))
                    tok = fin_rows[:, h * QT:(h + 1) * QT, TOK]
                    nc.vector.tensor_scalar(fsm[:, :], tok, 0.0, float(2 * N), ALU.is_equal, ALU.mult)
                    dve.drain()
                    nc.vector.scalar_tensor_tensor(fidx[:, h, :], tok, -1.0, fsm[:, :], ALU.add, ALU.add)
                    for i in range(QT):
                        y = n * QT + i
                        row = fin_rows[:, h * QT + i, :]
                        dve.wait_ge(f_y, y + 1)
                        if i == 0 and q % QUADS == 0:
                            dve.wait_ge(s_ew[q // QUADS], pair * 48 + 48)
                        t, big_, r = guard[:, i % 2, :], guard[:, 2 + i % 2, :], guard[:, 4 + i % 2, :]
                        fin = masks[:, i % 2, :]
                        nc.vector.tensor_tensor(t, ps[:, 5 + i % 2, 0:D], b2s[:, q // QUADS, :],
                                                ALU.add).then_inc(f_yread, 1)
                        dve.drain()
                        nc.vector.tensor_scalar(t, t, row[:, PRB:PRB + 1], None, ALU.mult)
                        dve.drain()
                        nc.vector.tensor_scalar(fin, t, 0.0, 0.0, ALU.mult, ALU.is_equal)
                        nc.vector.tensor_scalar(big_, t, FLT_MAX, 1e4, ALU.is_gt, ALU.mult)
                        nc.vector.tensor_scalar(r, t, -FLT_MAX, -1e4, ALU.is_lt, ALU.mult)
                        dve.drain()
                        nc.vector.tensor_tensor(r, r, big_, ALU.add)
                        dve.drain()
                        nc.vector.copy_predicated(r, fin, t)
                        dve.drain()
                        nc.vector.tensor_tensor(res[:, h * QT + i, :], r, row[:, 0:D], ALU.add).then_inc(f_res, 1)
            turns(dve, NE // 2, finish)

        @block.scalar
        def _(act):
            def root(g, h, var_ready, done):
                act.wait_ge(var_ready, g + 1)
                nc.scalar.activation(sd[:, h, :], ve[:, h, :], ACT.Sqrt).then_inc(done, 1)

            root(0, 0, s_var, s_sd)

            def support(it):
                for h in range(2):
                    for j in range(GB):
                        if j == 2 and not (isinstance(it, int) and it * 2 + h == LASTG):
                            root(it * 2 + h + 1, 1 - h, s_var, s_sd)
                        n = (it * 2 + h) * GB + j
                        r = (h * GB + j) % 2
                        act.wait_ge(s_xt, n + 1)
                        since(act, s_sp, n - 1)
                        nc.scalar.activation(xTs[:, r * KD:(r + 1) * KD, :],
                                             ps[:, 4 + r, 0:D].rearrange("p (k n) -> p k n", k=KD), ACT.Copy).then_inc(s_xts, 1)
                        act.wait_ge(s_sp, n + 1)
                        act.sem_inc(a_taken, 1)
                        nc.scalar.activation(S[:, bass.ds(n, 1), :].rearrange("p a d -> p (a d)"), ps[:, 6 + r, 0:D], ACT.Copy)\
                            .then_inc(s_S, 1)
            turns(act, GROUPS // 2, support)

            act.wait_ge(s_tables, 1)
            is_sorted = act.value_load(flag_i[0:1, 0:1], min_val=0, max_val=1)
            with act.If(is_sorted > 0):
                def take_g(s, r):
                    act.wait_ge(s_g, s + 1)
                    since(act, s_m, s - 3)
                    nc.scalar.activation(gsb[:, r, :], ps[:, 4 + r % 2, 0:P], ACT.Copy)\
                        .then_inc(s_gs, 1)

                take_g(0, 0)

                def rows(it):
                    last = isinstance(it, int) and it == ITER - 1
                    for k in range(U):
                        s = it * U + k
                        if not (last and k == U - 1):
                            take_g(s + 1, (k + 1) % 4)
                        act.wait_ge(s_m, s + 1)
                        if not isinstance(s, int) or s >= 8:
                            act.wait_ge(s_chain[k % CHAINS], (it * (U // CHAINS) + k // CHAINS + 1) * 16)
                        nc.scalar.activation(msg[:, k % 8, :], ps[:, 6 + k % 2, 0:D], ACT.Copy).then_inc(s_msg, 1)
                turns(act, ITER, rows)
            with act.Else():
                with act.Fori(0, STEPS) as s:
                    act.wait_ge(u_m, s + 1)
                    nc.scalar.activation(msg[:, 0, :], ps[:, 4, 0:D], ACT.Copy).then_inc(u_msg, 1)
                act.nop()

            def route(it):
                for h in range(2):
                    q = it * 2 + h
                    root(q, h, r_var, r_sd)
                    act.wait_ge(r_rs, q + 1)

                    def norm(j):
                        n = q * GB + j
                        r = (h * GB + j) % 2
                        since(act, r_xt, n - 1)
                        if not (isinstance(n, int) and n < 2):
                            act.sem_inc(a_taken, 1)
                        row = lambda lo, hi: xr[:, bass.ds(n, 1), lo:hi].rearrange("p a d -> p (a d)")
                        nc.scalar.activation(rxn[:, r, :], row(0, D), ACT.Identity, bias=row(NMR, NMR + 1),
                                             scale=row(RSTD, RSTD + 1)).then_inc(r_xn, 1)

                    norm(0)
                    for j in range(GB):
                        n = q * GB + j
                        r = (h * GB + j) % 2
                        if j + 1 < GB:
                            norm(j + 1)
                        act.wait_ge(r_xt, n + 1)
                        since(act, r_lg, n - 1)
                        nc.scalar.activation(rxT[:, r * KD:(r + 1) * KD, :],
                                             ps[:, r, 0:D].rearrange("p (k n) -> p k n", k=KD), ACT.Copy).then_inc(r_xts, 1)
                    act.wait_ge(r_l, q + 1)
                    nc.scalar.activation(lg[:, h, :, :], lg[:, h, :, :], ACT.Exp).then_inc(r_ex, 1)
            turns(act, GROUPS // 2, route)

            act.wait_ge(s_routed, 1)

            def norm_quad(n, turn, h):
                act.wait_ge(s_rows[h], turn * 16 + 16)
                for i in range(QT):
                    if i == 0:
                        since(act, f_xt, n)
                    row = fin_rows[:, h * QT + i, :]
                    nc.scalar.activation(fxn[:, i, :], row[:, 0:D], ACT.Identity, bias=row[:, NMR:NMR + 1],
                                         scale=row[:, RSTD:RSTD + 1]).then_inc(f_xn, 1)

            norm_quad(0, 0, 0)

            def hidden(pair):
                last = isinstance(pair, int) and pair == NE // 2 - 1
                for q in range(2 * QUADS):
                    n = pair * (2 * QUADS) + q
                    for f in range(KF):
                        m = n * KF + f
                        act.wait_ge(f_h, m + 1)
                        if f == 0:
                            since(act, f_y, (n - 1) * QT)
                        e = pair * 2 + q // QUADS
                        act.sem_inc(a_taken, 1)
                        nc.scalar.activation(hT[:, (q % 2) * KF + f, :], ps[:, HB[f % 4], :], ACT.Relu,
                                             bias=b1s[:, bass.ds(e, 1), f]).then_inc(f_hs, 1)
                        if f == 3 and not (last and q == 2 * QUADS - 1):
                            norm_quad(n + 1, pair * QUADS + (q + 1) // 2, (q + 1) % 2)
            turns(act, NE // 2, hidden)

        @block.tensor
        def _(pe):
            pe.wait_ge(s_const, 15)
            pe.wait_ge(s_late, 1)
            nc.tensor.matmul(ps[:, 0, 0:1], ones[:, :], late[:, 0:1], start=True, stop=True).then_inc(s_latesum, 1)
            for c in range(TC):
                pe.wait_ge(s_oh, c + 1)
                since(pe, s_selread, c - 1)
                for n, table in enumerate((srcR, dstR, wR, None)):
                    for t in ([c - 1] if c else []) + [c]:
                        rows = table[:, t, :] if table is not None else tvals[:, t:t + 1].to_broadcast([P, P])
                        last = nc.tensor.matmul(ps[:, 1 + c % 2, n * P:(n + 1) * P], rows,
                                                OH[:, t, (c - t) * P:(c - t + 1) * P],
                                                start=t == max(c - 1, 0), stop=t == c)
                last.then_inc(s_sel, 1)

            pe.wait_ge(s_w, 16)

            def support(it):
                for h in range(2):
                    def transpose(j):
                        n = (it * 2 + h) * GB + j
                        r = (h * GB + j) % 2
                        pe.wait_ge(s_xn, n + 1)
                        since(pe, s_xts, n - 1)
                        for k in range(KD):
                            last = nc.tensor.transpose(ps[:, 4 + r, k * P:(k + 1) * P], xin[:, h * GB + j, k * P:(k + 1) * P],
                                                       ident[:, :])
                        last.then_inc(s_xt, 1)

                    transpose(0)
                    for j in range(GB):
                        n = (it * 2 + h) * GB + j
                        r = (h * GB + j) % 2
                        if j + 1 < GB:
                            transpose(j + 1)
                        pe.wait_ge(s_xts, n + 1)
                        since(pe, s_S, n - 1)
                        for k in range(KD):
                            last = nc.tensor.matmul(ps[:, 6 + r, 0:D], xTs[:, r * KD + k, :], Ws[:, k, :],
                                                    start=k == 0, stop=k == KD - 1)
                        last.then_inc(s_sp, 1)
            turns(pe, GROUPS // 2, support)

            pe.wait_ge(s_tables, 1)
            pe.wait_ge(s_S, BLOCKS)
            is_sorted = pe.value_load(flag_i[0:1, 0:1], min_val=0, max_val=1)
            with pe.If(is_sorted > 0):
                def src_row(it, k):
                    s = it * U + k
                    half, c = k // 8 % 2, k % 8
                    if c == 0:
                        pe.wait_ge(s_col, it * 2 + k // 8 + 1)
                    since(pe, s_eq, s - 3)
                    nc.tensor.transpose(ps[:, k % 4, 0:P],
                                        colring[:, half, c, 0:1].to_broadcast([P, P]), ident[:, :]).then_inc(s_srow, 1)

                def g_of(s, r):
                    pe.wait_ge(s_ohw, s + 1)
                    since(pe, s_gs, s - 1)
                    nc.tensor.matmul(ps[:, 4 + r % 2, 0:P], ohw[:, r, :], eqs[:, r, :],
                                     start=True, stop=True).then_inc(s_g, 1)

                for k in range(3):
                    src_row(0, k)
                g_of(0, 0)

                def steps(it):
                    last = isinstance(it, int) and it == ITER - 1
                    for k in range(U):
                        s = it * U + k
                        if k % 4 == 0:
                            packed = pe.value_load(bpack[0:1, bass.ds(it * (U // 4) + k // 4, 1)], min_val=0,
                                                   max_val=(1 << 28) - 1)
                        if not (last and k + 3 >= U):
                            src_row(it, k + 3)
                        if not (last and k == U - 1):
                            g_of(s + 1, (k + 1) % 4)
                        b = nc.s_assert_within((packed >> (7 * (k % 4))) & 127, 0, BLOCKS - 1,
                                               skip_runtime_bounds_check_because="i - t is a block of dst, or 0")
                        pe.wait_ge(s_gs, s + 1)
                        since(pe, s_msg, s - 1)
                        nc.tensor.matmul(ps[:, 6 + k % 2, 0:D], gsb[:, k % 4, :],
                                         S[:, bass.ds(b, 1), :].rearrange("p a d -> p (a d)"),
                                         start=True, stop=True).then_inc(s_m, 1)
                turns(pe, ITER, steps)
            with pe.Else():
                with pe.Fori(0, STEPS) as s:
                    pe.wait_ge(u_col, s + 1)
                    nc.tensor.transpose(ps[:, 0, 0:P], colring[:, 0, 0, 0:1].to_broadcast([P, P]), ident[:, :])\
                        .then_inc(u_srow, 1)
                    pe.wait_ge(u_idx, s + 1)
                    pe.wait_ge(u_rows, s * 16 + 16)
                    nc.tensor.matmul(ps[:, 4, 0:D], eqs[:, 0, :], msg[:, 1, :], start=True, stop=True).then_inc(u_m, 1)
                pe.nop()

            pe.wait_ge(s_gate, 48)
            pe.wait_ge(s_graph, 1)

            def route(it):
                for h in range(2):
                    q = it * 2 + h

                    def transpose(j):
                        n = q * GB + j
                        r = (h * GB + j) % 2
                        pe.wait_ge(r_xn, n + 1)
                        since(pe, r_xts, n - 1)
                        for k in range(KD):
                            last = nc.tensor.transpose(ps[:, r, k * P:(k + 1) * P], rxn[:, r, k * P:(k + 1) * P], ident[:, :])
                        last.then_inc(r_xt, 1)

                    transpose(0)
                    for j in range(GB):
                        n = q * GB + j
                        r = (h * GB + j) % 2
                        if j + 1 < GB:
                            transpose(j + 1)
                        pe.wait_ge(r_xts, n + 1)
                        if j == 0:
                            since(pe, r_l, q)
                        for k in range(KD):
                            last = nc.tensor.matmul(ps[:, 4, j * NE:(j + 1) * NE], rxT[:, r * KD + k, :], gws[:, k, :],
                                                    start=k == 0, stop=k == KD - 1)
                        last.then_inc(r_lg, 1)
                    pe.wait_ge(r_cum, q + 1)
                    count = ps[:, 5, 0:NE * GB].rearrange("p (e j) -> p e j", e=NE)
                    nc.tensor.matmul(count, before[:, :], ohx[:, :, 1:GB + 1], start=True, stop=False)
                    nc.tensor.matmul(count, ones[:, :], cum[:, :, 0:GB], start=False, stop=True).then_inc(r_pos, 1)
            turns(pe, GROUPS // 2, route)

            def quad_T(n):
                since(pe, f_xts, n)
                for i in range(QT):
                    pe.wait_ge(f_xn, n * QT + i + 1)
                    for k in range(KD):
                        last = nc.tensor.transpose(ps[:, 3 + k, i * P:(i + 1) * P], fxn[:, i, k * P:(k + 1) * P], ident[:, :])
                last.then_inc(f_xt, 1)

            quad_T(0)

            def layers(pair):
                last_pair = isinstance(pair, int) and pair == NE // 2 - 1
                for q in range(2 * QUADS):
                    n = pair * (2 * QUADS) + q
                    h, e = q % 2, q // QUADS
                    pe.wait_ge(f_xts, n + 1)
                    if q % QUADS == 0:
                        pe.wait_ge(s_ew[e], pair * 48 + 48)
                    for f in range(KF):
                        since(pe, f_hs, n * KF + f - 3)
                        for k in range(KD):
                            last = nc.tensor.matmul(ps[:, HB[f % 4], :], w1s[:, e * KD + k, f * P:(f + 1) * P],
                                                    fxT[:, h * KD + k, :], start=k == 0, stop=k == KD - 1)
                        last.then_inc(f_h, 1)
                    if not (last_pair and q == 2 * QUADS - 1):
                        quad_T(n + 1)
                    pe.wait_ge(f_hs, n * KF + KF)
                    for i in range(QT):
                        since(pe, f_yread, n * QT + i - 1)
                        for f in range(KF):
                            last = nc.tensor.matmul(ps[:, 5 + i % 2, 0:D],
                                                    hT[:, h * KF + f, i * P:(i + 1) * P], w2s[:, e * KF + f, :],
                                                    start=f == 0, stop=f == KF - 1)
                        last.then_inc(f_y, 1)
            turns(pe, NE // 2, layers)


_INS = ['x', 'src', 'dst', 'edge_weight', 'L0_gnn_W', 'L0_ffn_gate_w', 'L0_ffn_gate_b', 'L0_ffn_w1', 'L0_ffn_b1',
        'L0_ffn_w2', 'L0_ffn_b2']


def kernel(**inputs):
    import numpy as _np
    import concourse.bacc as _bacc
    from concourse import mybir as _mybir
    from concourse.bass_utils import run_bass_kernel_spmd as _run

    nc = _bacc.Bacc("TRN2", target_bir_lowering=False, num_devices=1)
    arrays, args = {}, []
    for name in _INS:
        a = _np.ascontiguousarray(inputs[name])
        arrays[f"in_{name}_dram"] = a
        args.append(nc.dram_tensor(f"in_{name}_dram", a.shape, _mybir.dt.from_np(a.dtype), kind="ExternalInput").ap())
    shape = inputs["x"].shape
    args.append(nc.dram_tensor("out_0_dram", shape, _mybir.dt.float32, kind="ExternalOutput").ap())
    bass_gnn_then_top1_ffn(nc, *args)
    r = _run(nc, [arrays], core_ids=[0])
    return r.results[0]["out_0_dram"]
```

```python
import concourse.bass as bass
from concourse import mybir
from contextlib import ExitStack


def bass_gnn_then_top1_ffn(
    nc: bass.Bass,
    x: bass.AP,
    src: bass.AP,
    dst: bass.AP,
    edge_weight: bass.AP,
    gnn_w: bass.AP,
    gate_w: bass.AP,
    gate_b: bass.AP,
    w1: bass.AP,
    b1: bass.AP,
    w2: bass.AP,
    b2: bass.AP,
    out: bass.AP,
):
    f32 = mybir.dt.float32
    i32 = mybir.dt.int32
    u32 = mybir.dt.uint32
    ALU = mybir.AluOpType
    ACT = mybir.ActivationFunctionType
    AX = mybir.AxisListType

    P = 128
    N, D = x.shape
    E = src.shape[0]
    NE = gate_w.shape[1]
    F = w1.shape[2]
    KD = D // P
    KF = F // P
    EPS = 1e-5
    FLT_MAX = 3.4028234663852886e38

    BLOCKS = -(-N // P)
    LASTROWS = N - (BLOCKS - 1) * P
    GB = 7
    GROUPS = BLOCKS // GB
    assert GROUPS * GB == BLOCKS and GROUPS % 2 == 0 and GROUPS >= 6

    TILES = -(-E // P)
    TC = -(-(TILES + BLOCKS - 1) // P)
    STEPS = TC * P
    FULLT = E // P
    TAILE = E - FULLT * P
    U = 16
    ITER = STEPS // U
    CHAINS = 4
    assert STEPS % U == 0 and (TC - 1) * P <= FULLT and BLOCKS <= P and TAILE > 0

    SPLIT = 4
    PIECES = 11
    PACE = 4
    DUMP = N
    ACCR = 99
    ACCROWS = P * ACCR
    assert ACCROWS >= max(N + P, BLOCKS * P) and ACCR % PIECES == 0 and N * D % (P * (PIECES - 1)) == 0

    CAP = max(1, -(-5 * N // (4 * NE)))
    SLOTS = -(-CAP // 512) * 512
    QT = 4
    QUADS = SLOTS // (QT * P)
    XW = D + 4
    RSTD, NMR, PRB, TOK = D, D + 1, D + 2, D + 3
    TRASH = NE * SLOTS
    assert QUADS % 2 == 0 and NE % 2 == 0

    acc = [nc.dram_tensor(f"acc{c}", (ACCROWS, D), f32).ap() for c in range(CHAINS)]
    support_dram = nc.dram_tensor("support_dram", (BLOCKS * P, D), f32).ap()
    buf = nc.dram_tensor("buf", (TRASH, XW), f32).ap()

    ctx = ExitStack()
    with ctx:
        def sb(name, shape, dt=f32):
            return ctx.enter_context(nc.sbuf_tensor(name, shape, dt))

        def sem(name):
            return ctx.enter_context(nc.semaphore(name))

        big = sb("big", [P, BLOCKS * XW])
        work = sb("work", [P, 12288])
        cols = sb("cols", [P, STEPS, 3])
        pre = sb("pre", [P, 5120])

        def view(region, at, *shape):
            size = 1
            for n in shape:
                size *= n
            v = region[:, at:at + size]
            if len(shape) == 2:
                v = v.rearrange("p (a b) -> p a b", a=shape[0])
            if len(shape) == 3:
                v = v.rearrange("p (a b c) -> p a b c", a=shape[0], b=shape[1])
            return v, at + size

        S, _ = view(big, 0, BLOCKS, D)
        xr, _ = view(big, 0, BLOCKS, XW)
        hT, at = view(big, 0, 2 * KF, QT * P)
        fin_rows, at = view(big, at, 2 * QT, XW)
        fxn, at = view(big, at, QT, D)
        fxT, at = view(big, at, 2 * KD, QT * P)
        res, at = view(big, at, 2 * QT, D)
        guard, at = view(big, at, 6, D)
        masks, at = view(big, at, 2, D)
        masks = masks.bitcast(i32)
        assert at <= BLOCKS * XW
        srcR, at = view(work, 0, TC, P)
        dstR, at = view(work, at, TC, P)
        dstS, at = view(work, at, TC, P)
        wR, at = view(work, at, TC, P)
        OH, at = view(work, at, TC, 2 * P)
        btab = work[0:1, at:at + STEPS].bitcast(i32)
        bpack = work[0:1, at + STEPS:at + STEPS + STEPS // 4].bitcast(i32)
        bpart = work[0:1, 0:STEPS // 2].bitcast(i32).rearrange("a (n k) -> a n k", n=2)
        assert at + STEPS + STEPS // 4 <= 12288
        msg, at = view(work, 0, 8, D)
        gsb, at = view(work, at, 4, P)
        ohw, at = view(work, at, 4, P)
        eqs, at = view(work, at, 4, P)
        junk, at = view(work, at, 2, P)
        w1s, at = view(work, 0, 2 * KD, F)
        w2s, at = view(work, at, 2 * KF, D)
        b2s, at = view(work, at, 2, D)
        assert at <= 12288
        xin, at = view(pre, 0, 2 * GB, D)
        xTs, at = view(pre, at, 2 * KD, P)
        rxn, at = view(pre, 0, 2, D)
        rxT, at = view(pre, at, 2 * KD, P)
        assert at <= 5120

        iota_i = sb("iota_i", [P, STEPS])
        ident = sb("ident", [P, P])
        ones = sb("ones", [P, P])
        before = sb("before", [P, P])
        dump_before = sb("dump_before", [P, P])
        dump_col = sb("dump_col", [P, 1])
        trash_col = sb("trash_col", [P, 1])
        tvals = sb("tvals", [P, TC])
        tokp1 = sb("tokp1", [P, BLOCKS])
        valid = sb("valid", [P, BLOCKS])
        zero = sb("zero", [P, 3 * D])
        Ws = sb("Ws", [P, KD, D])
        gws = sb("gws", [P, KD, NE])
        gbs = sb("gbs", [P, NE])
        b1s = sb("b1s", [P, NE, KF])
        scan_keep = sb("scan_keep", [P, NE, GB + 1])
        hi_i = sb("hi_i", [P, 2, TC], i32)
        keys = sb("keys", [P, 3, TC])
        late = sb("late", [P, 2])
        flag_f = sb("flag_f", [P, 1])
        flag_i = sb("flag_i", [P, 1], i32)
        brow = sb("brow", [P, 2, P])
        colring = sb("colring", [P, 2, 8, 3])
        dups = sb("dups", [P, 8])
        idxr = sb("idxr", [P, 8], u32)
        idxd = sb("idxd", [P, 1], u32)
        stats = sb("stats", [P, 2, GB, 6])
        mv = sb("mv", [P, 2, GB, 2])
        ve = sb("ve", [P, 2, GB])
        sd = sb("sd", [P, 2, GB])
        rs = sb("rs", [P, 2, GB])
        lg = sb("lg", [P, 2, GB, NE])
        pr = sb("pr", [P, 2, GB, NE])
        cand = sb("cand", [P, GB, NE])
        small = sb("small", [P, 8, GB])
        ohx = sb("ohx", [P, NE, GB + 1])
        cum = sb("cum", [P, NE, GB + 1])
        pos = sb("pos", [P, GB, NE])
        slots = sb("slots", [P, BLOCKS], u32)
        fidx = sb("fidx", [P, 2, QT], u32)
        fsm = sb("fsm", [P, QT])
        live = sb("live", [1, NE, QUADS])
        live_sum = sb("live_sum", [1, NE])
        live_bit = sb("live_bit", [1, QUADS, 2])
        live_pack = sb("live_pack", [1, NE // 2], i32)

        ps = ctx.enter_context(nc.psum_tensor("ps", [P, 8, 512], f32))
        HB = (0, 1, 2, 7)

        s_const = sem("s_const")
        s_edge = [sem(f"s_edge{i}") for i in range(4)]
        s_pad = sem("s_pad")
        s_w = sem("s_w")
        s_gate = sem("s_gate")
        s_xin = [sem(f"s_xin{i}") for i in range(2)]
        s_xtail = sem("s_xtail")
        s_chain = [sem(f"s_chain{c}") for c in range(CHAINS)]
        s_bufz = sem("s_bufz")
        v_step = sem("v_step")
        s_late = sem("s_late")
        s_latesum = sem("s_latesum")
        s_oh = sem("s_oh")
        s_sel = sem("s_sel")
        s_selread = sem("s_selread")
        s_tables = sem("s_tables")
        s_var = sem("s_var")
        s_sd = sem("s_sd")
        s_xn = sem("s_xn")
        s_xt = sem("s_xt")
        s_xts = sem("s_xts")
        s_sp = sem("s_sp")
        s_S = sem("s_S")
        s_col = sem("s_col")
        s_srow = sem("s_srow")
        s_eq = sem("s_eq")
        s_dup = sem("s_dup")
        s_ohw = sem("s_ohw")
        s_idx = sem("s_idx")
        s_g = sem("s_g")
        s_gs = sem("s_gs")
        s_m = sem("s_m")
        s_msg = sem("s_msg")
        s_taken = sem("s_taken")
        a_taken = sem("a_taken")
        u_turn = sem("u_turn")
        u_sup = sem("u_sup")
        u_col = sem("u_col")
        u_rows = sem("u_rows")
        u_srow = sem("u_srow")
        u_dup = sem("u_dup")
        u_idx = sem("u_idx")
        u_m = sem("u_m")
        u_msg = sem("u_msg")
        u_sent = sem("u_sent")
        s_graph = sem("s_graph")
        s_ld = [sem(f"s_ld{i}") for i in range(4)]
        s_sum = [sem(f"s_sum{i}") for i in range(4)]
        s_xr = sem("s_xr")
        r_var = sem("r_var")
        r_sd = sem("r_sd")
        r_rs = sem("r_rs")
        r_xn = sem("r_xn")
        r_xt = sem("r_xt")
        r_xts = sem("r_xts")
        r_lg = sem("r_lg")
        r_l = sem("r_l")
        r_ex = sem("r_ex")
        r_cum = sem("r_cum")
        r_pos = sem("r_pos")
        r_slot = sem("r_slot")
        s_disp = sem("s_disp")
        s_base = sem("s_base")
        s_routed = sem("s_routed")
        s_total = sem("s_total")
        s_live = sem("s_live")
        s_ew = [sem(f"s_ew{i}") for i in range(2)]
        s_rows = [sem(f"s_rows{i}") for i in range(2)]
        f_xn = sem("f_xn")
        f_xt = sem("f_xt")
        f_xts = sem("f_xts")
        f_h = sem("f_h")
        f_hs = sem("f_hs")
        f_y = sem("f_y")
        f_yread = sem("f_yread")
        f_res = sem("f_res")
        f_idx = sem("f_idx")
        f_v = sem("f_v")
        s_out = [sem(f"s_out{i}") for i in range(2)]

        block = ctx.enter_context(nc.Block())

        def since(eng, semaphore, count):
            if isinstance(count, int) and count <= 0:
                return
            eng.wait_ge(semaphore, count)

        def turns(eng, n, body):
            body(0)
            with eng.Fori(1, n - 1) as it:
                body(it)
            body(n - 1)

        def edge_rows(a, shift=0):
            n = (TC - 1) * P * P
            return a[0:n].rearrange("(c p e) -> p c e", p=P, e=P)

        x_groups = x[0:(GROUPS - 1) * GB * P, :].rearrange("(g j p) d -> g p j d", j=GB, p=P)
        LASTG = GROUPS - 1

        @block.sync
        def _(sp):
            sp.dma_start(Ws[:, :, :], gnn_w.rearrange("(k p) n -> p k n", p=P)).then_inc(s_w, 16)

            def load_edges():
                tabs = [(src, srcR.bitcast(i32)), (dst, dstR.bitcast(i32)), (edge_weight, wR)]
                sp.wait_ge(s_pad, 4)
                tail0 = (TC - 1) * P
                rows = FULLT - tail0
                for i, (a, r) in enumerate(tabs):
                    sp.dma_start(r[:, 0:TC - 1, :], edge_rows(a)).then_inc(s_edge[i], 16)
                    sp.dma_start(r[0:rows, TC - 1, :],
                                 a[tail0 * P:FULLT * P].rearrange("(p e) -> p e", e=P)).then_inc(s_edge[i], 16)
                    sp.dma_start(r[rows:rows + 1, TC - 1, 0:TAILE],
                                 a[FULLT * P:E].rearrange("(p e) -> p e", p=1)).then_inc(s_edge[i], 16)
                sh = dstS.bitcast(i32)
                sp.dma_start(sh[0:1, 0, 1:P], dst[0:P - 1].rearrange("(p e) -> p e", p=1)).then_inc(s_edge[3], 16)
                sp.dma_start(sh[1:P, 0, :], dst[P - 1:P * P - 1].rearrange("(p e) -> p e", e=P)).then_inc(s_edge[3], 16)
                sp.dma_start(sh[:, 1:TC - 1, :],
                             dst[P * P - 1:(TC - 1) * P * P - 1].rearrange("(c p e) -> p c e", p=P, e=P))\
                  .then_inc(s_edge[3], 16)
                sp.dma_start(sh[0:rows, TC - 1, :],
                             dst[tail0 * P - 1:FULLT * P - 1].rearrange("(p e) -> p e", e=P)).then_inc(s_edge[3], 16)
                sp.dma_start(sh[rows:rows + 1, TC - 1, 0:TAILE],
                             dst[FULLT * P - 1:E - 1].rearrange("(p e) -> p e", p=1)).then_inc(s_edge[3], 16)

            def load_x(it):
                for h in range(2):
                    last = isinstance(it, int) and 2 * it + h == LASTG
                    since(sp, s_xt, (it * 2 + h - 1) * GB)
                    if not last:
                        sp.dma_start(xin[:, h * GB:(h + 1) * GB, :],
                                     x_groups[bass.ds(it * 2 + h, 1), :, :, :].rearrange("a p j d -> p (a j) d"))\
                          .then_inc(s_xin[h], 16)
                        continue
                    at = LASTG * GB * P
                    sp.dma_start(xin[:, h * GB:(h + 1) * GB - 1, :],
                                 x[at:at + (GB - 1) * P, :].rearrange("(j p) d -> p j d", p=P)).then_inc(s_xin[h], 16)
                    sp.dma_start(xin[0:LASTROWS, (h + 1) * GB - 1, :], x[N - LASTROWS:N, :]).then_inc(s_xtail, 16)
                    sp.dma_start(xin[LASTROWS:P, (h + 1) * GB - 1, :], zero[0:P - LASTROWS, 0:D]).then_inc(s_xtail, 16)

            sp.wait_ge(s_const, 1)
            load_x(0)
            load_edges()
            with sp.Fori(1, GROUPS // 2 - 1) as it:
                load_x(it)
            load_x(GROUPS // 2 - 1)
            sp.dma_start(gws[:, :, :], gate_w.rearrange("(k p) n -> p k n", p=P)).then_inc(s_gate, 16)
            sp.dma_start(gbs[:, :], gate_b.rearrange("(a n) -> a n", a=1).to_broadcast([P, NE])).then_inc(s_gate, 16)
            flat = buf.rearrange("r w -> (r w)").rearrange("(p q f) -> p q f", p=P, f=TRASH * XW // P // 65)
            sp.dma_start(flat, zero[:, 0:flat.shape[2]].rearrange("p (a f) -> p a f", a=1)
                         .to_broadcast([P, 65, flat.shape[2]])).then_inc(s_bufz, 16)
            with nc.allow_non_contiguous_dma(reason="expert biases by column, once"):
                sp.dma_start(b1s[:, :, :], b1.rearrange("e (f p) -> p e f", p=P)).then_inc(s_gate, 16)

            sp.wait_ge(s_graph, 1)

            def load_expert(e, h):
                sp.dma_start(w1s[:, h * KD:(h + 1) * KD, :],
                             w1[bass.ds(e, 1), :, :].rearrange("a (k p) f -> p (a k) f", p=P)).then_inc(s_ew[h], 16)
                sp.dma_start(w2s[:, h * KF:(h + 1) * KF, :],
                             w2[bass.ds(e, 1), :, :].rearrange("a (k p) d -> p (a k) d", p=P)).then_inc(s_ew[h], 16)
                sp.dma_start(b2s[:, h, :], b2[bass.ds(e, 1), :].to_broadcast([P, D])).then_inc(s_ew[h], 16)

            load_expert(0, 0)
            for q in range(GROUPS + 4):
                if q >= 4:
                    g = q - 4
                    sp.wait_ge(s_xr, g + 1)
                    rows = GB if g < LASTG else GB - 1
                    sp.dma_start(out[g * GB * P:(g * GB + rows) * P, :].rearrange("(j p) d -> p j d", p=P),
                                 xr[:, g * GB:g * GB + rows, 0:D]).then_inc(s_base, 16)
                if q < GROUPS:
                    sp.dma_start(xr[:, q * GB:(q + 1) * GB, 0:D],
                                 acc[0][q * GB * P:(q + 1) * GB * P, :].rearrange("(j p) d -> p j d", p=P))\
                      .then_inc(s_ld[q % 4], 16)
            sp.dma_start(out[N - LASTROWS:N, :], xr[0:LASTROWS, BLOCKS - 1, 0:D]).then_inc(s_base, 16)
            sp.wait_ge(s_routed, 1)

            def ffn_loads(pair):
                for q in range(2 * QUADS):
                    n = pair * (2 * QUADS) + q
                    since(sp, f_res, (n - 1) * QT)
                    row = n * (QT * P)
                    sp.dma_start(fin_rows[:, (q % 2) * QT:(q % 2 + 1) * QT, :],
                                 buf[bass.ds(row, QT * P), :].rearrange("(i p) w -> p i w", p=P))\
                      .then_inc(s_rows[q % 2], 16)
                    if q == 0:
                        since(sp, f_res, pair * (2 * QUADS * QT))
                        load_expert(pair * 2 + 1, 1)
                    if q == QUADS and not (isinstance(pair, int) and pair == NE // 2 - 1):
                        sp.wait_ge(f_res, pair * (2 * QUADS * QT) + QUADS * QT)
                        load_expert(pair * 2 + 2, 0)

            turns(sp, NE // 2, ffn_loads)

        @block.gpsimd
        def _(pool):
            pool.memset(zero[:, :], 0.0).then_inc(s_const, 1)
            c = TC - 1
            pool.iota(srcR.bitcast(i32)[:, c, :], pattern=[[1, P]], base=DUMP, channel_multiplier=0).then_inc(s_pad, 1)
            pool.memset(dstR.bitcast(i32)[:, c, :], N - 1).then_inc(s_pad, 1)
            pool.memset(dstS.bitcast(i32)[:, c, :], N - 1).then_inc(s_pad, 1)
            pool.memset(wR[:, c, :], 0.0).then_inc(s_pad, 1)
            pool.memset(dstS.bitcast(i32)[0:1, 0, 0:1], 0).then_inc(s_const, 1)
            pool.memset(ones[:, :], 1.0).then_inc(s_const, 1)
            pool.memset(ident[:, :], 0.0).then_inc(s_const, 1)
            pool.memset(scan_keep[:, :, :], 1.0).then_inc(s_const, 1)
            pool.iota(iota_i[:, :], pattern=[[1, STEPS]], base=0, channel_multiplier=0,
                      allow_small_or_imprecise_dtypes=True).then_inc(s_const, 1)
            pool.iota(tvals[:, :], pattern=[[P, TC]], base=0, channel_multiplier=1,
                      allow_small_or_imprecise_dtypes=True).then_inc(s_const, 1)
            pool.iota(tokp1[:, :], pattern=[[P, BLOCKS]], base=1, channel_multiplier=1,
                      allow_small_or_imprecise_dtypes=True).then_inc(s_const, 1)
            pool.iota(dump_col[:, :], pattern=[[0, 1]], base=DUMP, channel_multiplier=1,
                      allow_small_or_imprecise_dtypes=True).then_inc(s_const, 1)
            pool.iota(trash_col[:, :], pattern=[[0, 1]], base=TRASH, channel_multiplier=1,
                      allow_small_or_imprecise_dtypes=True).then_inc(s_const, 1)
            pool.iota(dump_before[:, :], pattern=[[0, P]], base=DUMP, channel_multiplier=1,
                      allow_small_or_imprecise_dtypes=True).then_inc(s_const, 1)
            pool.wait_ge(s_const, 11)
            pool.affine_select(out=ident[:, :], in_=ident[:, :], compare_op=ALU.not_equal, fill=1.0, base=0,
                               pattern=[[-1, P]], channel_multiplier=1).then_inc(s_const, 1)
            pool.affine_select(out=before[:, :], in_=ones[:, :], compare_op=ALU.is_gt, fill=0.0, base=0,
                               pattern=[[1, P]], channel_multiplier=-1).then_inc(s_const, 1)
            pool.affine_select(out=dump_before[:, :], in_=dump_before[:, :], compare_op=ALU.is_gt, fill=0.0, base=0,
                               pattern=[[-1, P]], channel_multiplier=1).then_inc(s_const, 1)
            pool.memset(scan_keep[:, :, 0:1], 0.0).then_inc(s_const, 1)

            tail = (ACCROWS - N) * D // P
            flat_x = x.rearrange("r d -> (r d)").rearrange("(q p f) -> q p f", p=P, q=PIECES - 1)
            flat_0 = acc[0][0:N, :].rearrange("r d -> (r d)").rearrange("(q p f) -> q p f", p=P, q=PIECES - 1)
            for n in range(PIECES):
                for a in range(CHAINS):
                    count = n * CHAINS + a
                    if 0 < count * PACE <= BLOCKS:
                        pool.wait_ge(s_xt, count * PACE)
                    if a:
                        rows = acc[a][n * ACCROWS // PIECES:(n + 1) * ACCROWS // PIECES, :]
                        pool.dma_start(rows.rearrange("(p q r) d -> p q (r d)", p=P, r=3),
                                       zero[:, :].rearrange("p (a f) -> p a f", a=1)
                                       .to_broadcast([P, ACCR // PIECES // 3, 3 * D])).then_inc(s_chain[a], 16)
                    elif n < PIECES - 1:
                        pool.dma_start(flat_0[n, :, :], flat_x[n, :, :]).then_inc(s_chain[0], 16)
                    else:
                        pool.dma_start(acc[0][N:ACCROWS, :].rearrange("r d -> (r d)").rearrange("(p f) -> p f", p=P),
                                       zero[:, 0:tail]).then_inc(s_chain[0], 16)
                    if count == SPLIT * 2 * GB // PACE - 1:
                        pool.wait_ge(s_late, 1)
                        pool.partition_all_reduce(late[:, 1:2], late[:, 0:1], P, bass.bass_isa.ReduceOp.add)\
                            .then_inc(s_latesum, 1)

            def add_rows(a, col, rows, done):
                pool.sem_inc(s_taken, 1)
                pool.indirect_dma_start(out=acc[a], out_offset=bass.IndirectOffsetOnAxis(ap=col, axis=0),
                                        in_=rows, in_offset=None, compute_op=ALU.add).then_inc(done, 16)

            pool.wait_ge(s_tables, 1)
            is_sorted = pool.value_load(flag_i[0:1, 0:1], min_val=0, max_val=1)
            with pool.If(is_sorted > 0):
                def scatter(it):
                    for k in range(U):
                        s = it * U + k
                        pool.wait_ge(s_msg, s + 1)
                        pool.wait_ge(s_idx, s + 1)
                        pool.wait_ge(s_chain[k % CHAINS], (it * (U // CHAINS) + k // CHAINS + PIECES) * 16)
                        add_rows(k % CHAINS, idxr[:, k % 8:k % 8 + 1], msg[:, k % 8, :], s_chain[k % CHAINS])
                turns(pool, ITER, scatter)
                for a in range(CHAINS):
                    pool.wait_ge(s_chain[a], 16 * (PIECES + STEPS // CHAINS))
                pool.nop().then_inc(s_graph, 1)
            with pool.Else():
                pool.wait_ge(s_S, BLOCKS)
                for a in range(CHAINS):
                    pool.wait_ge(s_chain[a], 16 * PIECES)
                pool.dma_start(support_dram.rearrange("(j p) d -> p j d", p=P), S[:, :, :]).then_inc(u_sup, 16)
                pool.wait_ge(u_sup, 16)
                pool.nop().then_inc(u_turn, 1)
                with pool.Fori(0, STEPS) as s:
                    pool.wait_ge(u_col, s + 1)
                    pool.sem_inc(s_taken, 1)
                    pool.indirect_dma_start(out=msg[:, 1, :], out_offset=None, in_=support_dram,
                                            in_offset=bass.IndirectOffsetOnAxis(ap=idxd[:, 0:1], axis=0))\
                        .then_inc(u_rows, 16)
                    pool.wait_ge(u_msg, s + 1)
                    add_rows(0, idxr[:, 0:1], msg[:, 0, :], u_sent)
                    pool.wait_ge(u_sent, s * 16 + 16)
                    pool.sem_inc(u_turn, 1)
                pool.nop().then_inc(s_graph, 1)

            for w in range(GROUPS + 6):
                for stage in range(CHAINS, 0, -1):
                    q = w - stage
                    if not 0 <= q < GROUPS:
                        continue
                    if stage == 1:
                        pool.wait_ge(s_ld[q % 4], 16 * (q // 4 + 1))
                    else:
                        pool.wait_ge(s_sum[q % 4], 16 * ((CHAINS - 1) * (q // 4) + stage - 1))
                    if stage == CHAINS:
                        pool.nop().then_inc(s_xr, 1)
                        continue
                    pool.dma_start(xr[:, q * GB:(q + 1) * GB, 0:D],
                                   acc[stage][q * GB * P:(q + 1) * GB * P, :].rearrange("(j p) d -> p j d", p=P),
                                   accum_op=ALU.add).then_inc(s_sum[q % 4], 16)
                q = w - 6
                if q < 0:
                    continue
                if q == 0:
                    pool.wait_ge(s_bufz, 16)
                pool.wait_ge(r_slot, q + 1)
                for j in range(q * GB, (q + 1) * GB):
                    pool.indirect_dma_start(out=buf, out_offset=bass.IndirectOffsetOnAxis(ap=slots[:, j:j + 1], axis=0),
                                            in_=xr[:, j, :], in_offset=None, bounds_check=TRASH - 1,
                                            oob_is_err=False).then_inc(s_disp, 16)
            pool.wait_ge(s_disp, 16 * BLOCKS)
            pool.wait_ge(s_base, 16 * (GROUPS + 1))
            pool.nop().then_inc(s_routed, 1)

            def send(pair):
                for q in range(2 * QUADS):
                    n = pair * (2 * QUADS) + q
                    for i in range(QT):
                        pool.wait_ge(f_res, n * QT + i + 1)
                        pool.sem_inc(s_taken, 1)
                        pool.indirect_dma_start(out=out, out_offset=bass.IndirectOffsetOnAxis(ap=fidx[:, q % 2, i:i + 1], axis=0),
                                                in_=res[:, (q % 2) * QT + i, :], in_offset=None,
                                                bounds_check=N - 1, oob_is_err=False).then_inc(s_out[q % 2], 16)
            turns(pool, NE // 2, send)
            for h in range(2):
                pool.wait_ge(s_out[h], 16 * NE * QUADS * QT // 2)

        @block.vector
        def _(dve):
            chain = [0]

            def link(ins):
                chain[0] += 1
                ins.then_inc(v_step, 1)
                dve.wait_ge(v_step, chain[0])

            srcI, dstI, dstSI = (a.bitcast(i32) for a in (srcR, dstR, dstS))
            def norm_stats(rows, h, var_ready):
                for j in range(GB):
                    nc.vector.bn_stats(stats[:, h, j, :], rows(j))
                dve.drain()
                for j in range(GB):
                    nc.vector.bn_aggr(mv[:, h, j, :], stats[:, h, j, :])
                dve.drain()
                nc.vector.tensor_scalar(ve[:, h, :], mv[:, h, :, 1], EPS, None, ALU.add).then_inc(var_ready, 1)

            def norm_x(it):
                for h in range(2):
                    dve.wait_ge(s_xin[h], it * 16 + 16)
                    if isinstance(it, int) and 2 * it + h == LASTG:
                        dve.wait_ge(s_xtail, 32)
                    norm_stats(lambda j: xin[:, h * GB + j, :], h, s_var)
                    dve.wait_ge(s_sd, it * 2 + h + 1)
                    nc.vector.reciprocal(rs[:, h, :], sd[:, h, :])
                    dve.drain()
                    for j in range(GB):
                        nc.vector.tensor_scalar(xin[:, h * GB + j, :], xin[:, h * GB + j, :], mv[:, h, j, 0:1],
                                                rs[:, h, j:j + 1], ALU.subtract, ALU.mult).then_inc(s_xn, 1)
            def edge_tables():
                dve.wait_ge(s_const, 15)
                for i in range(3):
                    dve.wait_ge(s_edge[i], 48)
                dve.wait_ge(s_edge[3], 80)
                nc.vector.tensor_scalar(hi_i[:, 0, :], dstI[:, :, P - 1], 7, None, ALU.arith_shift_right)
                link(nc.vector.tensor_scalar(hi_i[:, 1, :], dstSI[:, :, 0], 7, None, ALU.arith_shift_right))
                nc.vector.tensor_copy(keys[:, 0:2, :], hi_i[:, :, :])
                nc.vector.tensor_copy(srcR[:, :, :], srcI[:, :, :])
                nc.vector.tensor_copy(dstR[:, :, :], dstI[:, :, :])
                link(nc.vector.tensor_copy(dstS[:, :, :], dstSI[:, :, :]))
                nc.vector.tensor_scalar(valid[:, :], tokp1[:, :], float(N), None, ALU.is_le)
                link(nc.vector.tensor_tensor(OH[:, :, 0:P], dstS[:, :, :], dstR[:, :, :], ALU.is_gt))
                nc.vector.tensor_reduce(late[:, 0:1], OH[:, :, 0:P], AX.XY, ALU.add).then_inc(s_late, 1)
                dve.wait_ge(s_latesum, 1)
                link(nc.vector.tensor_scalar(flag_f[:, :], late[:, 1:2], 0.0, None, ALU.is_equal))
                nc.vector.tensor_copy(flag_i[:, :], flag_f[:, :])
                nc.vector.scalar_tensor_tensor(keys[:, 2, :], keys[:, 0, :], flag_f[:, 0:1], tvals[:, :], ALU.mult, ALU.add)
                link(nc.vector.scalar_tensor_tensor(keys[:, 1, :], keys[:, 1, :], flag_f[:, 0:1], tvals[:, :],
                                                    ALU.mult, ALU.add))
                link(nc.vector.tensor_scalar(keys[:, 1, :], keys[:, 1, :], 1.0, None, ALU.subtract))
                for c in range(TC):
                    n = 2 * P if c < TC - 1 else P
                    link(nc.vector.tensor_scalar(OH[:, c, 0:n], iota_i[:, c * P:c * P + n], keys[:, 1, c:c + 1], None, ALU.is_gt))
                    nc.vector.scalar_tensor_tensor(OH[:, c, 0:n], iota_i[:, c * P:c * P + n], keys[:, 2, c:c + 1],
                                                   OH[:, c, 0:n], ALU.is_le, ALU.mult).then_inc(s_oh, 1)

            norm_x(0)
            with dve.Fori(1, SPLIT) as it:
                norm_x(it)
            edge_tables()
            with dve.Fori(SPLIT, GROUPS // 2 - 1) as it:
                norm_x(it)
            norm_x(GROUPS // 2 - 1)


            for c in range(TC):
                dve.wait_ge(s_sel, c + 1)
                bank = ps[:, 1 + c % 2, :]
                i0 = c * P
                nc.vector.tensor_copy(cols[:, i0:i0 + P, 0], bank[:, 0:P])
                nc.vector.tensor_copy(cols[:, i0:i0 + P, 2], bank[:, 2 * P:3 * P])
                link(nc.vector.scalar_tensor_tensor(brow[:, c % 2, :], bank[:, 3 * P:4 * P], -1.0, iota_i[:, i0:i0 + P],
                                                    ALU.mult, ALU.add))
                nc.vector.tensor_copy(btab[0:1, i0:i0 + P], brow[0:1, c % 2, :])
                nc.vector.scalar_tensor_tensor(cols[:, i0:i0 + P, 1], brow[:, c % 2, :], float(-P), bank[:, P:2 * P],
                                               ALU.mult, ALU.add).then_inc(s_selread, 1)
            dve.wait_ge(s_selread, TC)
            quad = btab[0:1, :].rearrange("a (n k) -> a n k", k=4)
            link(nc.vector.tensor_copy(bpack[0:1, :], quad[:, :, 0]))
            for k in range(1, 4):
                link(nc.vector.tensor_scalar(bpart[0:1, k % 2, :], quad[:, :, k], 7 * k, None, ALU.logical_shift_left))
                link(nc.vector.tensor_tensor(bpack[0:1, :], bpack[0:1, :], bpart[0:1, k % 2, :], ALU.bitwise_or))
            nc.vector.memset(ohx[:, :, 0:1], 0.0).then_inc(s_tables, 1)

            is_sorted = dve.value_load(flag_i[0:1, 0:1], min_val=0, max_val=1)
            with dve.If(is_sorted > 0):
                dve.wait_ge(s_S, BLOCKS)

                def take_cols(half, n):
                    nc.vector.tensor_copy(colring[:, half, :, :], cols[:, bass.ds(n * 8, 8), :]).then_inc(s_col, 1)

                take_cols(0, 0)

                def edges(it):
                    last = isinstance(it, int) and it == ITER - 1
                    for k in range(U):
                        s = it * U + k
                        half, c = k // 8, k % 8
                        if k == 4:
                            take_cols(1, it * 2 + 1)
                        if k == 12 and not last:
                            take_cols(0, it * 2 + 2)
                        if c == 0:
                            dve.wait_ge(s_col, it * 2 + half + 1)
                        src_c, dst_c, w_c = (colring[:, half, c, n:n + 1] for n in range(3))
                        dve.wait_ge(s_srow, s + 1)
                        row = ps[:, k % 4, 0:P]
                        nc.vector.scalar_tensor_tensor(junk[:, k % 2, :], row, src_c, dump_before[:, :],
                                                       ALU.is_equal, ALU.mult, accum_out=dups[:, c:c + 1])\
                            .then_inc(s_dup, 1)
                        since(dve, s_g, s - 3)
                        nc.vector.tensor_scalar(eqs[:, k % 4, :], row, src_c, None, ALU.is_equal).then_inc(s_eq, 1)
                        nc.vector.tensor_scalar(ohw[:, k % 4, :], iota_i[:, 0:P], dst_c, w_c, ALU.is_equal, ALU.mult)\
                            .then_inc(s_ohw, 1)
                        if not isinstance(s, int) or s >= 8:
                            dve.wait_ge(s_chain[k % CHAINS], (it * (U // CHAINS) + k // CHAINS + PIECES - 1) * 16)
                        dve.wait_ge(s_dup, s + 1)
                        nc.vector.tensor_scalar(idxr[:, c:c + 1], dups[:, c:c + 1], src_c, dump_col[:, 0:1],
                                                ALU.max, ALU.min).then_inc(s_idx, 1)
                turns(dve, ITER, edges)
            with dve.Else():
                dve.wait_ge(s_S, BLOCKS)
                with dve.Fori(0, STEPS) as s:
                    dve.wait_ge(u_turn, s + 1)
                    nc.vector.tensor_copy(idxd[:, 0:1], cols[:, bass.ds(s, 1), 1])
                    nc.vector.tensor_copy(colring[:, 0, 0:1, :], cols[:, bass.ds(s, 1), :]).then_inc(u_col, 1)
                    dve.wait_ge(u_srow, s + 1)
                    nc.vector.scalar_tensor_tensor(junk[:, 0, :], ps[:, 0, 0:P], colring[:, 0, 0, 0:1], dump_before[:, :],
                                                   ALU.is_equal, ALU.mult, accum_out=dups[:, 0:1]).then_inc(u_dup, 1)
                    nc.vector.tensor_scalar(eqs[:, 0, :], ps[:, 0, 0:P], colring[:, 0, 0, 0:1], colring[:, 0, 0, 2:3],
                                            ALU.is_equal, ALU.mult)
                    dve.wait_ge(u_dup, s + 1)
                    nc.vector.tensor_scalar(idxr[:, 0:1], dups[:, 0:1], colring[:, 0, 0, 0:1], dump_col[:, 0:1],
                                            ALU.max, ALU.min).then_inc(u_idx, 1)
                dve.nop()

            dve.wait_ge(s_graph, 1)
            dve.wait_ge(s_gate, 48)

            def norm_group(q, h):
                    dve.wait_ge(s_xr, q + 1)
                    norm_stats(lambda j: xr[:, bass.ds(q * GB + j, 1), 0:D].rearrange("p a d -> p (a d)"), h, r_var)
                    dve.wait_ge(r_sd, q + 1)
                    group = lambda c: xr[:, bass.ds(q * GB, GB), c]
                    nc.vector.reciprocal(rs[:, h, :], sd[:, h, :])
                    dve.drain()
                    nc.vector.tensor_copy(group(RSTD), rs[:, h, :])
                    nc.vector.scalar_tensor_tensor(small[:, 0, :], mv[:, h, :, 0], -1.0, rs[:, h, :], ALU.mult, ALU.mult)
                    dve.drain()
                    nc.vector.tensor_copy(group(NMR), small[:, 0, :])
                    nc.vector.tensor_copy(group(TOK), tokp1[:, bass.ds(q * GB, GB)]).then_inc(r_rs, 1)

            norm_group(0, 0)

            def route(it):
                for h in range(2):
                    q = it * 2 + h
                    if not (isinstance(it, int) and q == LASTG):
                        norm_group(q + 1, 1 - h)
                    group = lambda c: xr[:, bass.ds(q * GB, GB), c]
                    wide = lambda a: a.rearrange("p (j a) -> p j a", a=1).to_broadcast([P, GB, NE])
                    over_j = lambda a: a.rearrange("p (a e) -> p a e", a=1).to_broadcast([P, GB, NE])
                    dve.wait_ge(r_lg, (q + 1) * GB)
                    logit = ps[:, 6 + h, 0:GB * NE].rearrange("p (j e) -> p j e", e=NE)
                    nc.vector.tensor_tensor(lg[:, h, :, :], logit, over_j(gbs[:, :]), ALU.add)
                    dve.drain()
                    nc.vector.tensor_reduce(small[:, 1, :], lg[:, h, :, :], AX.X, ALU.max)
                    dve.drain()
                    nc.vector.tensor_tensor(lg[:, h, :, :], lg[:, h, :, :], wide(small[:, 1, :]), ALU.subtract)\
                        .then_inc(r_l, 1)
                    dve.wait_ge(r_ex, q + 1)
                    nc.vector.tensor_reduce(small[:, 2, :], lg[:, h, :, :], AX.X, ALU.add)
                    dve.drain()
                    nc.vector.reciprocal(small[:, 3, :], small[:, 2, :])
                    dve.drain()
                    nc.vector.tensor_tensor(pr[:, h, :, :], lg[:, h, :, :], wide(small[:, 3, :]), ALU.mult)
                    dve.drain()
                    nc.vector.tensor_reduce(small[:, 4, :], pr[:, h, :, :], AX.X, ALU.max)
                    dve.drain()
                    nc.vector.tensor_copy(group(PRB), small[:, 4, :])
                    nc.vector.tensor_tensor(cand[:, :, :], pr[:, h, :, :], wide(small[:, 4, :]), ALU.is_equal)
                    dve.drain()
                    nc.vector.scalar_tensor_tensor(cand[:, :, :], cand[:, :, :], float(-NE), over_j(iota_i[:, 0:NE]),
                                                   ALU.mult, ALU.add)
                    dve.drain()
                    nc.vector.tensor_reduce(small[:, 5, :], cand[:, :, :], AX.X, ALU.min)
                    dve.drain()
                    nc.vector.tensor_tensor(cand[:, :, :], cand[:, :, :], wide(small[:, 5, :]), ALU.is_equal)
                    dve.drain()
                    chosen = ohx[:, :, 1:GB + 1].rearrange("p e j -> p j e")
                    nc.vector.tensor_tensor(chosen, cand[:, :, :], wide(valid[:, bass.ds(q * GB, GB)]), ALU.mult)
                    dve.drain()
                    nc.vector.tensor_tensor_scan(cum[:, :, :].rearrange("p e j -> p (e j)"),
                                                 scan_keep[:, :, :].rearrange("p e j -> p (e j)"),
                                                 ohx[:, :, :].rearrange("p e j -> p (e j)"), 0.0, ALU.mult, ALU.add)\
                        .then_inc(r_cum, 1)
                    dve.wait_ge(r_pos, q + 1)
                    count = ps[:, 5, 0:NE * GB].rearrange("p (e j) -> p j e", e=NE)
                    nc.vector.tensor_tensor(pos[:, :, :], count, chosen, ALU.mult)
                    nc.vector.tensor_scalar(small[:, 5, :], small[:, 5, :], float(NE), float(SLOTS), ALU.add, ALU.mult)
                    dve.drain()
                    nc.vector.tensor_reduce(small[:, 6, :], pos[:, :, :], AX.X, ALU.add)
                    nc.vector.tensor_copy(ohx[:, :, 0:1], cum[:, :, GB:GB + 1])
                    dve.drain()
                    nc.vector.scalar_tensor_tensor(small[:, 7, :], small[:, 6, :], float(CAP), valid[:, bass.ds(q * GB, GB)],
                                                   ALU.is_lt, ALU.mult)
                    nc.vector.scalar_tensor_tensor(small[:, 6, :], small[:, 6, :], trash_col[:, 0:1], small[:, 5, :],
                                                   ALU.subtract, ALU.add)
                    dve.drain()
                    nc.vector.tensor_tensor(small[:, 6, :], small[:, 6, :], small[:, 7, :], ALU.mult)
                    dve.drain()
                    nc.vector.tensor_scalar(slots[:, bass.ds(q * GB, GB)], small[:, 6, :], trash_col[:, 0:1], None, ALU.add)\
                        .then_inc(r_slot, 1)
            turns(dve, GROUPS // 2, route)

            first = live_bit[:, :, 0]
            nc.vector.tensor_scalar(first, iota_i[0:1, 0:QUADS], float(QT * P), None, ALU.mult)
            for q in range(QUADS):
                nc.vector.memset(live_bit[:, q:q + 1, 1], float(1 << q))
            dve.wait_ge(s_total, 1)
            dve.drain()
            nc.vector.tensor_tensor(live[:, :, :], ps[0:1, 5, 0:NE].rearrange("a (e q) -> a e q", q=1).to_broadcast([1, NE, QUADS]),
                                    live_bit[:, :, 0:1].rearrange("a q k -> a k q").to_broadcast([1, NE, QUADS]), ALU.is_gt)
            dve.drain()
            nc.vector.tensor_tensor(live[:, :, :], live[:, :, :],
                                    live_bit[:, :, 1:2].rearrange("a q k -> a k q").to_broadcast([1, NE, QUADS]), ALU.mult)
            dve.drain()
            nc.vector.tensor_reduce(live_sum[:, :], live[:, :, :], AX.X, ALU.add)
            dve.drain()
            nc.vector.scalar_tensor_tensor(live_pack[:, :], live_sum[:, 1:NE:2], float(1 << QUADS), live_sum[:, 0:NE:2],
                                           ALU.mult, ALU.add).then_inc(s_live, 1)

            dve.wait_ge(s_routed, 1)
            dve.wait_ge(s_live, 1)

            def take_xT(n, h):
                dve.wait_ge(f_xt, n + 1)
                nc.vector.tensor_copy(fxT[:, h * KD:(h + 1) * KD, :], ps[:, 3:3 + KD, :]).then_inc(f_xts, 1)

            take_xT(0, 0)

            def finish(pair):
                last = isinstance(pair, int) and pair == NE // 2 - 1
                holds = dve.value_load(live_pack[0:1, bass.ds(pair, 1)], min_val=0, max_val=(1 << 2 * QUADS) - 1)
                for q in range(2 * QUADS):
                    n = pair * (2 * QUADS) + q
                    h = q % 2
                    if not (last and q == 2 * QUADS - 1):
                        take_xT(n + 1, 1 - h)
                    since(dve, s_out[h], (pair * QUADS + q // 2) * (16 * QT))
                    tok = fin_rows[:, h * QT:(h + 1) * QT, TOK]
                    nc.vector.tensor_scalar(fsm[:, :], tok, 0.0, float(2 * N), ALU.is_equal, ALU.mult)
                    dve.drain()
                    nc.vector.scalar_tensor_tensor(fidx[:, h, :], tok, -1.0, fsm[:, :], ALU.add, ALU.add)
                    if q % QUADS == 0:
                        dve.wait_ge(s_ew[q // QUADS], pair * 48 + 48)
                    with dve.If(((holds >> q) & 1) > 0):
                        for i in range(QT):
                            y = n * QT + i
                            row = fin_rows[:, h * QT + i, :]
                            dve.wait_ge(f_y, y + 1)
                            t, big_, r = guard[:, i % 2, :], guard[:, 2 + i % 2, :], guard[:, 4 + i % 2, :]
                            fin = masks[:, i % 2, :]
                            nc.vector.tensor_tensor(t, ps[:, 5 + i % 2, 0:D], b2s[:, q // QUADS, :],
                                                    ALU.add).then_inc(f_yread, 1)
                            dve.drain()
                            nc.vector.tensor_scalar(t, t, row[:, PRB:PRB + 1], None, ALU.mult)
                            dve.drain()
                            nc.vector.tensor_scalar(fin, t, 0.0, 0.0, ALU.mult, ALU.is_equal)
                            nc.vector.tensor_scalar(big_, t, FLT_MAX, 1e4, ALU.is_gt, ALU.mult)
                            nc.vector.tensor_scalar(r, t, -FLT_MAX, -1e4, ALU.is_lt, ALU.mult)
                            dve.drain()
                            nc.vector.tensor_tensor(r, r, big_, ALU.add)
                            dve.drain()
                            nc.vector.copy_predicated(r, fin, t)
                            dve.drain()
                            nc.vector.tensor_tensor(res[:, h * QT + i, :], r, row[:, 0:D], ALU.add).then_inc(f_res, 1)
                    with dve.Else():
                        dve.drain().then_inc(f_yread, QT)
                        dve.drain().then_inc(f_res, QT)
            turns(dve, NE // 2, finish)

        @block.scalar
        def _(act):
            def root(g, h, var_ready, done):
                act.wait_ge(var_ready, g + 1)
                nc.scalar.activation(sd[:, h, :], ve[:, h, :], ACT.Sqrt).then_inc(done, 1)

            root(0, 0, s_var, s_sd)

            def take_xT(n, r):
                act.wait_ge(s_xt, n + 1)
                since(act, s_sp, n - 1)
                nc.scalar.activation(xTs[:, r * KD:(r + 1) * KD, :],
                                     ps[:, 4 + r, 0:D].rearrange("p (k n) -> p k n", k=KD), ACT.Copy).then_inc(s_xts, 1)

            take_xT(0, 0)

            def support(it):
                for h in range(2):
                    for j in range(GB):
                        last = isinstance(it, int) and it * 2 + h == LASTG
                        if j == 2 and not last:
                            root(it * 2 + h + 1, 1 - h, s_var, s_sd)
                        n = (it * 2 + h) * GB + j
                        r = (h * GB + j) % 2
                        if not (last and j == GB - 1):
                            take_xT(n + 1, 1 - r)
                        act.wait_ge(s_sp, n + 1)
                        act.sem_inc(a_taken, 1)
                        nc.scalar.activation(S[:, bass.ds(n, 1), :].rearrange("p a d -> p (a d)"), ps[:, 6 + r, 0:D], ACT.Copy)\
                            .then_inc(s_S, 1)
            turns(act, GROUPS // 2, support)

            act.wait_ge(s_tables, 1)
            is_sorted = act.value_load(flag_i[0:1, 0:1], min_val=0, max_val=1)
            with act.If(is_sorted > 0):
                def take_g(s, r):
                    act.wait_ge(s_g, s + 1)
                    since(act, s_m, s - 3)
                    nc.scalar.activation(gsb[:, r, :], ps[:, 4 + r % 2, 0:P], ACT.Copy)\
                        .then_inc(s_gs, 1)

                take_g(0, 0)

                def rows(it):
                    last = isinstance(it, int) and it == ITER - 1
                    for k in range(U):
                        s = it * U + k
                        if not (last and k == U - 1):
                            take_g(s + 1, (k + 1) % 4)
                        act.wait_ge(s_m, s + 1)
                        if not isinstance(s, int) or s >= 8:
                            act.wait_ge(s_chain[k % CHAINS], (it * (U // CHAINS) + k // CHAINS + PIECES - 1) * 16)
                        nc.scalar.activation(msg[:, k % 8, :], ps[:, 6 + k % 2, 0:D], ACT.Copy).then_inc(s_msg, 1)
                turns(act, ITER, rows)
            with act.Else():
                with act.Fori(0, STEPS) as s:
                    act.wait_ge(u_m, s + 1)
                    nc.scalar.activation(msg[:, 0, :], ps[:, 4, 0:D], ACT.Copy).then_inc(u_msg, 1)
                act.nop()

            def exponents(q, h):
                act.wait_ge(r_l, q + 1)
                nc.scalar.activation(lg[:, h, :, :], lg[:, h, :, :], ACT.Exp).then_inc(r_ex, 1)

            root(0, 0, r_var, r_sd)

            def route(it):
                for h in range(2):
                    q = it * 2 + h
                    act.wait_ge(r_rs, q + 1)

                    def norm(j):
                        n = q * GB + j
                        r = (h * GB + j) % 2
                        since(act, r_xt, n - 1)
                        if not (isinstance(n, int) and n < 2):
                            act.sem_inc(a_taken, 1)
                        row = lambda lo, hi: xr[:, bass.ds(n, 1), lo:hi].rearrange("p a d -> p (a d)")
                        nc.scalar.activation(rxn[:, r, :], row(0, D), ACT.Identity, bias=row(NMR, NMR + 1),
                                             scale=row(RSTD, RSTD + 1)).then_inc(r_xn, 1)

                    norm(0)
                    for j in range(GB):
                        n = q * GB + j
                        r = (h * GB + j) % 2
                        if j + 1 < GB:
                            norm(j + 1)
                        if j == 1 and not (isinstance(q, int) and q == 0):
                            exponents(q - 1, 1 - h)
                        if j == GB - 2 and not (isinstance(q, int) and q == LASTG):
                            root(q + 1, 1 - h, r_var, r_sd)
                        act.wait_ge(r_xt, n + 1)
                        since(act, r_lg, n - 1)
                        nc.scalar.activation(rxT[:, r * KD:(r + 1) * KD, :],
                                             ps[:, r, 0:D].rearrange("p (k n) -> p k n", k=KD), ACT.Copy).then_inc(r_xts, 1)
            turns(act, GROUPS // 2, route)
            exponents(LASTG, LASTG % 2)

            act.wait_ge(s_routed, 1)
            act.wait_ge(s_live, 1)

            def norm_quad(n, turn, h):
                act.wait_ge(s_rows[h], turn * 16 + 16)
                for i in range(QT):
                    if i == 0:
                        since(act, f_xt, n)
                    row = fin_rows[:, h * QT + i, :]
                    nc.scalar.activation(fxn[:, i, :], row[:, 0:D], ACT.Identity, bias=row[:, NMR:NMR + 1],
                                         scale=row[:, RSTD:RSTD + 1]).then_inc(f_xn, 1)

            norm_quad(0, 0, 0)

            def hidden(pair):
                last = isinstance(pair, int) and pair == NE // 2 - 1
                holds = act.value_load(live_pack[0:1, bass.ds(pair, 1)], min_val=0, max_val=(1 << 2 * QUADS) - 1)
                for q in range(2 * QUADS):
                    n = pair * (2 * QUADS) + q
                    ahead = not (last and q == 2 * QUADS - 1)
                    with act.If(((holds >> q) & 1) > 0):
                        for f in range(KF):
                            act.wait_ge(f_h, n * KF + f + 1)
                            if f == 0:
                                since(act, f_y, (n - 1) * QT)
                            e = pair * 2 + q // QUADS
                            act.sem_inc(a_taken, 1)
                            nc.scalar.activation(hT[:, (q % 2) * KF + f, :], ps[:, HB[f % 4], :], ACT.Relu,
                                                 bias=b1s[:, bass.ds(e, 1), f]).then_inc(f_hs, 1)
                            if f == 3 and ahead:
                                norm_quad(n + 1, pair * QUADS + (q + 1) // 2, (q + 1) % 2)
                    with act.Else():
                        act.drain().then_inc(f_hs, KF)
                        if ahead:
                            norm_quad(n + 1, pair * QUADS + (q + 1) // 2, (q + 1) % 2)
                        act.nop()
            turns(act, NE // 2, hidden)

        @block.tensor
        def _(pe):
            pe.wait_ge(s_const, 15)
            pe.wait_ge(s_w, 16)

            def x_transpose(it, p):
                n = it * (2 * GB) + p
                p %= 2 * GB
                pe.wait_ge(s_xn, n + 1)
                since(pe, s_xts, n - 1)
                for k in range(KD):
                    last = nc.tensor.transpose(ps[:, 4 + p % 2, k * P:(k + 1) * P], xin[:, p, k * P:(k + 1) * P], ident[:, :])
                last.then_inc(s_xt, 1)

            x_transpose(0, 0)

            def support(it):
                for p in range(2 * GB):
                    n = it * (2 * GB) + p
                    if not (isinstance(it, int) and n == BLOCKS - 1):
                        x_transpose(it, p + 1)
                    pe.wait_ge(s_xts, n + 1)
                    since(pe, s_S, n - 1)
                    for k in range(KD):
                        last = nc.tensor.matmul(ps[:, 6 + p % 2, 0:D], xTs[:, p % 2 * KD + k, :], Ws[:, k, :],
                                                start=k == 0, stop=k == KD - 1)
                    last.then_inc(s_sp, 1)
            turns(pe, GROUPS // 2, support)

            for c in range(TC):
                pe.wait_ge(s_oh, c + 1)
                since(pe, s_selread, c - 1)
                for n, table in enumerate((srcR, dstR, wR, None)):
                    for t in ([c - 1] if c else []) + [c]:
                        rows = table[:, t, :] if table is not None else tvals[:, t:t + 1].to_broadcast([P, P])
                        last = nc.tensor.matmul(ps[:, 1 + c % 2, n * P:(n + 1) * P], rows,
                                                OH[:, t, (c - t) * P:(c - t + 1) * P],
                                                start=t == max(c - 1, 0), stop=t == c)
                last.then_inc(s_sel, 1)

            pe.wait_ge(s_tables, 1)
            pe.wait_ge(s_S, BLOCKS)
            is_sorted = pe.value_load(flag_i[0:1, 0:1], min_val=0, max_val=1)
            with pe.If(is_sorted > 0):
                def src_row(it, k):
                    s = it * U + k
                    half, c = k // 8 % 2, k % 8
                    if c == 0:
                        pe.wait_ge(s_col, it * 2 + k // 8 + 1)
                    since(pe, s_eq, s - 3)
                    nc.tensor.transpose(ps[:, k % 4, 0:P],
                                        colring[:, half, c, 0:1].to_broadcast([P, P]), ident[:, :]).then_inc(s_srow, 1)

                def g_of(s, r):
                    pe.wait_ge(s_ohw, s + 1)
                    since(pe, s_gs, s - 1)
                    nc.tensor.matmul(ps[:, 4 + r % 2, 0:P], ohw[:, r, :], eqs[:, r, :],
                                     start=True, stop=True).then_inc(s_g, 1)

                for k in range(3):
                    src_row(0, k)
                g_of(0, 0)

                def steps(it):
                    last = isinstance(it, int) and it == ITER - 1
                    for k in range(U):
                        s = it * U + k
                        if k % 4 == 0:
                            packed = pe.value_load(bpack[0:1, bass.ds(it * (U // 4) + k // 4, 1)], min_val=0,
                                                   max_val=(1 << 28) - 1)
                        if not (last and k + 3 >= U):
                            src_row(it, k + 3)
                        if not (last and k == U - 1):
                            g_of(s + 1, (k + 1) % 4)
                        b = nc.s_assert_within((packed >> (7 * (k % 4))) & 127, 0, BLOCKS - 1,
                                               skip_runtime_bounds_check_because="i - t is a block of dst, or 0")
                        pe.wait_ge(s_gs, s + 1)
                        since(pe, s_msg, s - 1)
                        nc.tensor.matmul(ps[:, 6 + k % 2, 0:D], gsb[:, k % 4, :],
                                         S[:, bass.ds(b, 1), :].rearrange("p a d -> p (a d)"),
                                         start=True, stop=True).then_inc(s_m, 1)
                turns(pe, ITER, steps)
            with pe.Else():
                with pe.Fori(0, STEPS) as s:
                    pe.wait_ge(u_col, s + 1)
                    nc.tensor.transpose(ps[:, 0, 0:P], colring[:, 0, 0, 0:1].to_broadcast([P, P]), ident[:, :])\
                        .then_inc(u_srow, 1)
                    pe.wait_ge(u_idx, s + 1)
                    pe.wait_ge(u_rows, s * 16 + 16)
                    nc.tensor.matmul(ps[:, 4, 0:D], eqs[:, 0, :], msg[:, 1, :], start=True, stop=True).then_inc(u_m, 1)
                pe.nop()

            pe.wait_ge(s_gate, 48)
            pe.wait_ge(s_graph, 1)

            def positions(q):
                pe.wait_ge(r_cum, q + 1)
                count = ps[:, 5, 0:NE * GB].rearrange("p (e j) -> p e j", e=NE)
                nc.tensor.matmul(count, before[:, :], ohx[:, :, 1:GB + 1], start=True, stop=False)
                nc.tensor.matmul(count, ones[:, :], cum[:, :, 0:GB], start=False, stop=True).then_inc(r_pos, 1)

            def route(it):
                for h in range(2):
                    q = it * 2 + h

                    def transpose(j):
                        n = q * GB + j
                        r = (h * GB + j) % 2
                        pe.wait_ge(r_xn, n + 1)
                        since(pe, r_xts, n - 1)
                        for k in range(KD):
                            last = nc.tensor.transpose(ps[:, r, k * P:(k + 1) * P], rxn[:, r, k * P:(k + 1) * P], ident[:, :])
                        last.then_inc(r_xt, 1)

                    transpose(0)
                    for j in range(GB):
                        n = q * GB + j
                        r = (h * GB + j) % 2
                        if j + 1 < GB:
                            transpose(j + 1)
                        pe.wait_ge(r_xts, n + 1)
                        if j == 0:
                            since(pe, r_l, q - 1)
                        if j == GB - 3 and not (isinstance(q, int) and q == 0):
                            positions(q - 1)
                        for k in range(KD):
                            last = nc.tensor.matmul(ps[:, 6 + h, j * NE:(j + 1) * NE], rxT[:, r * KD + k, :], gws[:, k, :],
                                                    start=k == 0, stop=k == KD - 1)
                        last.then_inc(r_lg, 1)
            turns(pe, GROUPS // 2, route)
            positions(LASTG)
            pe.wait_ge(r_slot, GROUPS)
            nc.tensor.matmul(ps[:, 5, 0:NE], ones[:, :], cum[:, :, GB], start=True, stop=True).then_inc(s_total, 1)

            pe.wait_ge(s_live, 1)

            def quad_T(n):
                since(pe, f_xts, n)
                for i in range(QT):
                    pe.wait_ge(f_xn, n * QT + i + 1)
                    for k in range(KD):
                        last = nc.tensor.transpose(ps[:, 3 + k, i * P:(i + 1) * P], fxn[:, i, k * P:(k + 1) * P], ident[:, :])
                last.then_inc(f_xt, 1)

            quad_T(0)

            def layers(pair):
                last_pair = isinstance(pair, int) and pair == NE // 2 - 1
                holds = pe.value_load(live_pack[0:1, bass.ds(pair, 1)], min_val=0, max_val=(1 << 2 * QUADS) - 1)
                for q in range(2 * QUADS):
                    n = pair * (2 * QUADS) + q
                    h, e = q % 2, q // QUADS
                    ahead = not (last_pair and q == 2 * QUADS - 1)
                    pe.wait_ge(f_xts, n + 1)
                    if q % QUADS == 0:
                        pe.wait_ge(s_ew[e], pair * 48 + 48)
                    with pe.If(((holds >> q) & 1) > 0):
                        for f in range(KF):
                            since(pe, f_hs, n * KF + f - 3)
                            for k in range(KD):
                                last = nc.tensor.matmul(ps[:, HB[f % 4], :], w1s[:, e * KD + k, f * P:(f + 1) * P],
                                                        fxT[:, h * KD + k, :], start=k == 0, stop=k == KD - 1)
                            last.then_inc(f_h, 1)
                        if ahead:
                            quad_T(n + 1)
                        pe.wait_ge(f_hs, n * KF + KF)
                        for i in range(QT):
                            since(pe, f_yread, n * QT + i - 1)
                            for f in range(KF):
                                last = nc.tensor.matmul(ps[:, 5 + i % 2, 0:D],
                                                        hT[:, h * KF + f, i * P:(i + 1) * P], w2s[:, e * KF + f, :],
                                                        start=f == 0, stop=f == KF - 1)
                            last.then_inc(f_y, 1)
                    with pe.Else():
                        pe.drain().then_inc(f_h, KF)
                        if ahead:
                            quad_T(n + 1)
                        pe.drain().then_inc(f_y, QT)
            turns(pe, NE // 2, layers)


_INS = ['x', 'src', 'dst', 'edge_weight', 'L0_gnn_W', 'L0_ffn_gate_w', 'L0_ffn_gate_b', 'L0_ffn_w1', 'L0_ffn_b1',
        'L0_ffn_w2', 'L0_ffn_b2']


def kernel(**inputs):
    import numpy as _np
    import concourse.bacc as _bacc
    from concourse import mybir as _mybir
    from concourse.bass_utils import run_bass_kernel_spmd as _run

    nc = _bacc.Bacc("TRN2", target_bir_lowering=False, num_devices=1)
    arrays, args = {}, []
    for name in _INS:
        a = _np.ascontiguousarray(inputs[name])
        arrays[f"in_{name}_dram"] = a
        args.append(nc.dram_tensor(f"in_{name}_dram", a.shape, _mybir.dt.from_np(a.dtype), kind="ExternalInput").ap())
    shape = inputs["x"].shape
    args.append(nc.dram_tensor("out_0_dram", shape, _mybir.dt.float32, kind="ExternalOutput").ap())
    bass_gnn_then_top1_ffn(nc, *args)
    r = _run(nc, [arrays], core_ids=[0])
    return r.results[0]["out_0_dram"]
```

```python
import concourse.bass as bass
from concourse import mybir
from contextlib import ExitStack


def bass_gnn_then_top1_ffn(
    nc: bass.Bass,
    x: bass.AP,
    src: bass.AP,
    dst: bass.AP,
    edge_weight: bass.AP,
    gnn_w: bass.AP,
    gate_w: bass.AP,
    gate_b: bass.AP,
    w1: bass.AP,
    b1: bass.AP,
    w2: bass.AP,
    b2: bass.AP,
    out: bass.AP,
):
    f32 = mybir.dt.float32
    i32 = mybir.dt.int32
    u32 = mybir.dt.uint32
    f32r = mybir.dt.float32r
    ALU = mybir.AluOpType
    ACT = mybir.ActivationFunctionType
    AX = mybir.AxisListType

    P = 128
    N, D = x.shape
    E = src.shape[0]
    NE = gate_w.shape[1]
    F = w1.shape[2]
    KD = D // P
    KF = F // P
    EPS = 1e-5
    FLT_MAX = 3.4028234663852886e38
    PASSES = ((0, 0), (0, 1), (1, 0))

    BLOCKS = -(-N // P)
    LASTROWS = N - (BLOCKS - 1) * P
    GB = 7
    GROUPS = BLOCKS // GB
    assert GROUPS * GB == BLOCKS and GROUPS % 2 == 0 and GROUPS >= 6

    TILES = -(-E // P)
    U = 16
    STEPS = -(-TILES // U) * U
    TC = -(-STEPS // P)
    FULLT = E // P
    TAILE = E - FULLT * P
    ITER = STEPS // U
    CHAINS = 4
    assert (TC - 1) * P <= FULLT and TAILE > 0

    STRIDE = 112
    SB = -(-N // STRIDE)
    SG = SB // GB
    LASTS = N - (SB - 1) * STRIDE
    assert SG * GB == SB and SG % 2 == 0 and SG >= 12 and SB <= P and STRIDE % 16 == 0
    DIV = -(-(1 << 16) // (STRIDE // 16))
    assert all(((n >> 4) * DIV) >> 16 == n // STRIDE for n in range(N)) and (N >> 4) * DIV < 1 << 24

    SPLIT = 4
    PIECES = 11
    PACE = 3
    BEHIND = 7
    DUMP = N
    ACCR = 99
    ACCROWS = P * ACCR
    assert ACCROWS >= max(N + P, BLOCKS * P) and ACCR % PIECES == 0 and N * D % (P * (PIECES - 1)) == 0

    CAP = max(1, -(-5 * N // (4 * NE)))
    SLOTS = -(-CAP // 512) * 512
    QT = 4
    QUADS = SLOTS // (QT * P)
    XW = D + 4
    RSTD, NMR, PRB, TOK = D, D + 1, D + 2, D + 3
    TRASH = NE * SLOTS
    WCH = 8
    BUF_PARTS = 13
    BUF_RUN = 512
    assert QUADS == 4 and NE % 2 == 0 and TRASH * XW % (P * BUF_PARTS * BUF_RUN) == 0

    acc = [nc.dram_tensor(f"acc{c}", (ACCROWS, D), f32).ap() for c in range(CHAINS)]
    support_dram = nc.dram_tensor("support_dram", (SB * STRIDE, D), f32).ap()
    buf = nc.dram_tensor("buf", (TRASH, XW), f32).ap()

    ctx = ExitStack()
    with ctx:
        def sb(name, shape, dt=f32):
            return ctx.enter_context(nc.sbuf_tensor(name, shape, dt))

        def sem(name):
            return ctx.enter_context(nc.semaphore(name))

        iota_i = sb("iota_i", [P, P])
        ident = sb("ident", [P, P])
        ones = sb("ones", [P, P])
        before = sb("before", [P, P])
        dump_before = sb("dump_before", [P, P])
        dump_col = sb("dump_col", [P, 1])
        trash_col = sb("trash_col", [P, 1])
        tokp1 = sb("tokp1", [P, BLOCKS])
        valid = sb("valid", [P, BLOCKS])
        zero = sb("zero", [P, 3 * D])
        Ws = sb("Ws", [P, KD, D])
        gws = sb("gws", [P, KD, NE])
        gbs = sb("gbs", [P, NE])
        b1s = sb("b1s", [P, NE, KF])
        scan_keep = sb("scan_keep", [P, NE, GB + 1])
        hi_i = sb("hi_i", [P, 2, TC], i32)
        keys = sb("keys", [P, 2, TC])
        late = sb("late", [P, 2])
        flag_f = sb("flag_f", [P, 1])
        flag_i = sb("flag_i", [P, 1], i32)
        colring = sb("colring", [P, 2, 8, 3])
        dups = sb("dups", [P, 8])
        idxr = sb("idxr", [P, 8], u32)
        idxd = sb("idxd", [P, 1], u32)
        stats = sb("stats", [P, 2, GB, 6])
        mv = sb("mv", [P, 2, GB, 2])
        ve = sb("ve", [P, 2, GB])
        sd = sb("sd", [P, 2, GB])
        rs = sb("rs", [P, 2, GB])
        lg = sb("lg", [P, 2, GB, NE])
        pr = sb("pr", [P, 2, GB, NE])
        cand = sb("cand", [P, GB, NE])
        small = sb("small", [P, 8, GB])
        ohx = sb("ohx", [P, NE, GB + 1])
        cum = sb("cum", [P, NE, GB + 1])
        pos = sb("pos", [P, GB, NE])
        slots = sb("slots", [P, BLOCKS], u32)
        fidx = sb("fidx", [P, QUADS, QT], u32)
        fsm = sb("fsm", [P, QT])
        live = sb("live", [1, NE, QUADS])
        live_sum = sb("live_sum", [1, NE])
        live_bit = sb("live_bit", [1, QUADS, 2])
        live_pack = sb("live_pack", [1, NE // 2], i32)

        early = ExitStack()

        def sb_early(name, shape, dt=f32):
            return early.enter_context(nc.sbuf_tensor(name, shape, dt))

        FRONT = max(9 * TC * P + STEPS + STEPS // 4 + SB * D - BLOCKS * XW - 3 * TC * P, 6 * KD * F + 2 * D)
        body = sb_early("body", [P, FRONT + BLOCKS * XW])
        pre = sb_early("pre", [P, 5120])

        def view(region, at, *shape):
            size = 1
            for n in shape:
                size *= n
            v = region[:, at:at + size]
            if len(shape) == 2:
                v = v.rearrange("p (a b) -> p a b", a=shape[0])
            if len(shape) == 3:
                v = v.rearrange("p (a b c) -> p a b c", a=shape[0], b=shape[1])
            return v, at + size

        xr, _ = view(body, FRONT, BLOCKS, XW)
        S, end = view(body, FRONT + BLOCKS * XW - SB * D, SB, D)
        cols, tables = view(body, 0, TC * P, 3)
        rel, at = view(body, 0, TC, P)
        outside, _ = view(body, at, TC, P)
        srcR, at = view(body, tables, TC, P)
        dstR, at = view(body, at, TC, P)
        wR, blocks = view(body, at, TC, P)
        btab = body[0:1, blocks:blocks + STEPS].bitcast(i32)
        bpack = body[0:1, blocks + STEPS:blocks + STEPS + STEPS // 4].bitcast(i32)
        bpart = body[0:1, tables:tables + STEPS // 2].bitcast(i32).rearrange("a (n k) -> a n k", n=2)
        assert blocks + STEPS + STEPS // 4 <= end - SB * D
        msg, at = view(body, tables, 8, D)
        gsb, at = view(body, at, 4, P)
        ohw, at = view(body, at, 4, P)
        eqs, at = view(body, at, 4, P)
        junk, at = view(body, at, 2, P)
        assert at <= blocks
        xin, at = view(pre, 0, 2 * GB, D)
        xTs, at = view(pre, at, 2 * KD, P)
        rxn, at = view(pre, 0, 2, D)
        rxT, at = view(pre, at, 2 * KD, P)
        assert at <= 5120

        early.close()
        w1p = [sb("w1p0", [P, 2, KD, F], f32r)]
        w2p = [sb("w2p0", [P, 2, KF, D], f32r)]
        w1s = sb("w1s", [P, KD, F])
        w2s = sb("w2s", [P, KF, D])
        b2s = sb("b2s", [P, 2, D])
        assert 6 * KD * F + 2 * D <= FRONT and KD * F == KF * D
        w1p.append(sb("w1p1", [P, 2, KD, F], f32r))
        w2p.append(sb("w2p1", [P, 2, KF, D], f32r))
        fin_rows = sb("fin_rows", [P, 4 * QT, XW])
        fxn = sb("fxn", [P, QT, D])
        fxT = sb("fxT", [P, 2, KD, QT * P], f32r)
        hT = sb("hT", [P, 2, KF, QT * P], f32r)
        h32 = sb("h32", [P, 4, QT * P])
        res = sb("res", [P, 2 * QT, D])
        guard = sb("guard", [P, 3, 2, D])
        masks = sb("masks", [P, 2, D], i32)

        ps = ctx.enter_context(nc.psum_tensor("ps", [P, 8, 512], f32))
        HB = (0, 1, 2, 7)

        s_const = sem("s_const")
        s_edge = [sem(f"s_edge{i}") for i in range(3)]
        s_pad = sem("s_pad")
        s_w = sem("s_w")
        s_gate = sem("s_gate")
        s_xin = [sem(f"s_xin{i}") for i in range(2)]
        s_xtail = sem("s_xtail")
        s_chain = [sem(f"s_chain{c}") for c in range(CHAINS)]
        s_bufz = sem("s_bufz")
        v_step = sem("v_step")
        s_late = sem("s_late")
        s_latesum = sem("s_latesum")
        s_tiles = sem("s_tiles")
        s_sel = sem("s_sel")
        s_selread = sem("s_selread")
        s_tables = sem("s_tables")
        s_var = sem("s_var")
        s_sd = sem("s_sd")
        s_xn = sem("s_xn")
        s_xt = sem("s_xt")
        s_xts = sem("s_xts")
        s_sp = sem("s_sp")
        s_S = sem("s_S")
        s_col = sem("s_col")
        s_srow = sem("s_srow")
        s_eq = sem("s_eq")
        s_dup = sem("s_dup")
        s_ohw = sem("s_ohw")
        s_idx = sem("s_idx")
        s_g = sem("s_g")
        s_gs = sem("s_gs")
        s_m = sem("s_m")
        s_msg = sem("s_msg")
        s_taken = sem("s_taken")
        a_taken = sem("a_taken")
        p_taken = sem("p_taken")
        u_turn = sem("u_turn")
        u_sup = sem("u_sup")
        u_col = sem("u_col")
        u_rows = sem("u_rows")
        u_srow = sem("u_srow")
        u_dup = sem("u_dup")
        u_idx = sem("u_idx")
        u_m = sem("u_m")
        u_msg = sem("u_msg")
        u_sent = sem("u_sent")
        s_graph = sem("s_graph")
        s_ld = [sem(f"s_ld{i}") for i in range(4)]
        s_sum = [sem(f"s_sum{i}") for i in range(4)]
        s_xr = sem("s_xr")
        r_var = sem("r_var")
        r_sd = sem("r_sd")
        r_rs = sem("r_rs")
        r_xn = sem("r_xn")
        r_xt = sem("r_xt")
        r_xts = sem("r_xts")
        r_lg = sem("r_lg")
        r_l = sem("r_l")
        r_ex = sem("r_ex")
        r_cum = sem("r_cum")
        r_pos = sem("r_pos")
        r_slot = sem("r_slot")
        s_disp = sem("s_disp")
        s_base = sem("s_base")
        s_routed = sem("s_routed")
        s_total = sem("s_total")
        s_resz = sem("s_resz")
        s_live = sem("s_live")
        s_ew = sem("s_ew")
        s_whi = sem("s_whi")
        s_wlo = sem("s_wlo")
        s_rows = [sem(f"s_rows{i}") for i in range(4)]
        f_xn = sem("f_xn")
        f_xt = sem("f_xt")
        f_xts = sem("f_xts")
        f_h = sem("f_h")
        f_hs = sem("f_hs")
        f_hl = sem("f_hl")
        f_y = sem("f_y")
        f_yread = sem("f_yread")
        f_res = sem("f_res")
        s_out = [sem(f"s_out{i}") for i in range(QUADS)]

        block = ctx.enter_context(nc.Block())

        def since(eng, semaphore, count):
            if isinstance(count, int) and count <= 0:
                return
            eng.wait_ge(semaphore, count)

        def holding(eng, holds, pair, q, prepare, skip):
            e, within = q // QUADS, q % QUADS
            exists = not (isinstance(pair, int) and pair == NE // 2 - 1 and e == 1)
            first = pair * (2 * QUADS) + (e + 1) * QUADS
            if within < QUADS - 1:
                with eng.If(((holds >> (q + 1)) & 1) > 0):
                    prepare(pair * (2 * QUADS) + q + 1, e, within + 1)
                    eng.nop()
                with eng.Else():
                    if exists:
                        skip(QUADS - 1 - within)
                        prepare(first, e + 1, 0)
                    eng.nop()
            elif exists:
                prepare(first, e + 1, 0)

        def turns(eng, n, body):
            body(0)
            with eng.Fori(1, n - 1) as it:
                body(it)
            body(n - 1)

        def edge_rows(a, shift=0):
            n = (TC - 1) * P * P
            return a[0:n].rearrange("(c p e) -> p c e", p=P, e=P)

        OVER = P - STRIDE
        x_groups = x[0:(SG - 1) * GB * STRIDE, :].rearrange("(g j p) d -> g p j d", j=GB, p=STRIDE)
        x_next = x[STRIDE:STRIDE + (SG - 1) * GB * STRIDE, :].rearrange("(g j p) d -> g p j d", j=GB, p=STRIDE)
        LASTG = GROUPS - 1

        @block.sync
        def _(sp):
            sp.dma_start(Ws[:, :, :], gnn_w.rearrange("(k p) n -> p k n", p=P)).then_inc(s_w, 16)

            def load_edges():
                tabs = [(src, srcR.bitcast(i32)), (dst, dstR.bitcast(i32)), (edge_weight, wR)]
                sp.wait_ge(s_pad, 3)
                tail0 = (TC - 1) * P
                rows = FULLT - tail0
                for i, (a, r) in enumerate(tabs):
                    sp.dma_start(r[:, 0:TC - 1, :], edge_rows(a)).then_inc(s_edge[i], 16)
                    sp.dma_start(r[0:rows, TC - 1, :],
                                 a[tail0 * P:FULLT * P].rearrange("(p e) -> p e", e=P)).then_inc(s_edge[i], 16)
                    sp.dma_start(r[rows:rows + 1, TC - 1, 0:TAILE],
                                 a[FULLT * P:E].rearrange("(p e) -> p e", p=1)).then_inc(s_edge[i], 16)
            def load_x(it):
                for h in range(2):
                    last = isinstance(it, int) and 2 * it + h == SG - 1
                    since(sp, s_xt, (it * 2 + h - 1) * GB)
                    if not last:
                        for rows, part in ((x_groups, slice(0, STRIDE)), (x_next, slice(STRIDE, P))):
                            sp.dma_start(xin[part, h * GB:(h + 1) * GB, :],
                                         rows[bass.ds(it * 2 + h, 1), 0:part.stop - part.start, :, :]
                                         .rearrange("a p j d -> p (a j) d")).then_inc(s_xin[h], 16)
                        continue
                    at = (SG - 1) * GB * STRIDE
                    end = (h + 1) * GB - 1
                    sp.dma_start(xin[0:STRIDE, h * GB:end, :],
                                 x[at:at + (GB - 1) * STRIDE, :].rearrange("(j p) d -> p j d", p=STRIDE)).then_inc(s_xin[h], 16)
                    sp.dma_start(xin[STRIDE:P, h * GB:end - 1, :],
                                 x[at + STRIDE:at + (GB - 1) * STRIDE, :].rearrange("(j p) d -> p j d", p=STRIDE)[0:OVER, :, :])\
                      .then_inc(s_xin[h], 16)
                    sp.dma_start(xin[STRIDE:P, end - 1, :], x[N - LASTS:N - LASTS + OVER, :]).then_inc(s_xtail, 16)
                    sp.dma_start(xin[0:LASTS, end, :], x[N - LASTS:N, :]).then_inc(s_xtail, 16)
                    sp.dma_start(xin[LASTS:P, end, :], zero[0:P - LASTS, 0:D]).then_inc(s_xtail, 16)

            sp.wait_ge(s_const, 1)
            load_x(0)
            load_edges()
            with sp.Fori(1, SG // 2 - 1) as it:
                load_x(it)
            load_x(SG // 2 - 1)
            sp.dma_start(gws[:, :, :], gate_w.rearrange("(k p) n -> p k n", p=P)).then_inc(s_gate, 16)
            sp.dma_start(gbs[:, :], gate_b.rearrange("(a n) -> a n", a=1).to_broadcast([P, NE])).then_inc(s_gate, 16)
            with nc.allow_non_contiguous_dma(reason="expert biases by column, once"):
                sp.dma_start(b1s[:, :, :], b1.rearrange("e (f p) -> p e f", p=P)).then_inc(s_gate, 16)

            flat = buf.rearrange("r w -> (r w)").rearrange("(n p q f) -> n p q f", n=BUF_PARTS, p=P, f=BUF_RUN)

            def clear_slots(n):
                sp.dma_start(flat[n, :, :, :], zero[:, 0:BUF_RUN].rearrange("p (a f) -> p a f", a=1)
                             .to_broadcast([P, flat.shape[2], BUF_RUN])).then_inc(s_bufz, 16)

            sp.wait_ge(s_tables, 1)
            is_local = sp.value_load(flag_i[0:1, 0:1], min_val=0, max_val=1)
            with sp.If(is_local > 0):
                for n in range(BUF_PARTS):
                    sp.wait_ge(s_col, 2 + n * (2 * ITER // BUF_PARTS))
                    clear_slots(n)
            with sp.Else():
                for n in range(BUF_PARTS):
                    clear_slots(n)
            sp.wait_ge(s_graph, 1)

            def load_expert(e, h):
                sp.dma_start(w1s[:, :, :], w1[bass.ds(e, 1), :, :].rearrange("a (k p) f -> p (a k) f", p=P)).then_inc(s_ew, 16)
                sp.dma_start(w2s[:, :, :], w2[bass.ds(e, 1), :, :].rearrange("a (k p) d -> p (a k) d", p=P)).then_inc(s_ew, 16)
                sp.dma_start(b2s[:, h, :], b2[bass.ds(e, 1), :].to_broadcast([P, D])).then_inc(s_ew, 16)

            for q in range(GROUPS + 4 + BEHIND):
                if q == 4:
                    load_expert(0, 0)
                if 4 <= q < GROUPS + 4:
                    sp.wait_ge(s_xr, q - 3)
                if q < GROUPS:
                    sp.dma_start(xr[:, q * GB:(q + 1) * GB, 0:D],
                                 acc[0][q * GB * P:(q + 1) * GB * P, :].rearrange("(j p) d -> p j d", p=P))\
                      .then_inc(s_ld[q % 4], 16)
                g = q - 4 - BEHIND
                if g >= 0:
                    rows = GB if g < LASTG else GB - 1
                    sp.dma_start(out[g * GB * P:(g * GB + rows) * P, :].rearrange("(j p) d -> p j d", p=P),
                                 xr[:, g * GB:g * GB + rows, 0:D]).then_inc(s_base, 16)
            sp.dma_start(out[N - LASTROWS:N, :], xr[0:LASTROWS, BLOCKS - 1, 0:D]).then_inc(s_base, 16)
            sp.wait_ge(s_routed, 1)

            def gate(semaphore, count):
                since(sp, semaphore, count)
                if not isinstance(count, int):
                    sp.sem_inc(p_taken, 1)

            def load_rows(pair, e, q):
                slot, used = e % 2 * 2 + q % 2, (pair + e // 2) * 2 + q // 2
                gate(s_rows[slot], used * 16)
                row = pair * (2 * SLOTS) + e * SLOTS + q * (QT * P)
                sp.dma_start(fin_rows[:, slot * QT:(slot + 1) * QT, :],
                             buf[bass.ds(row, QT * P), :].rearrange("(i p) w -> p i w", p=P)).then_inc(s_rows[slot], 16)

            load_rows(0, 0, 0)
            load_rows(0, 0, 1)

            def ffn_loads(pair):
                for e in range(2):
                    n = pair * (2 * QUADS) + e * QUADS
                    if not (isinstance(pair, int) and pair == NE // 2 - 1 and e):
                        gate(f_res, n * QT)
                        load_rows(pair, e + 1, 0)
                        load_rows(pair, e + 1, 1)
                        gate(s_wlo, pair * (2 * WCH) + (e + 1) * WCH)
                        load_expert(pair * 2 + e + 1, 1 - e)
                    for q in range(2, QUADS):
                        gate(f_res, (n + q - 1) * QT)
                        load_rows(pair, e, q)

            turns(sp, NE // 2, ffn_loads)
            for i in range(4):
                sp.wait_ge(s_rows[i], NE * QUADS // 4 * 16)

        @block.gpsimd
        def _(pool):
            pool.memset(zero[:, :], 0.0).then_inc(s_const, 1)
            c = TC - 1
            pool.iota(srcR.bitcast(i32)[:, c, :], pattern=[[1, P]], base=DUMP, channel_multiplier=0).then_inc(s_pad, 1)
            pool.memset(dstR.bitcast(i32)[:, c, :], N - 1).then_inc(s_pad, 1)
            pool.memset(wR[:, c, :], 0.0).then_inc(s_pad, 1)
            pool.memset(ones[:, :], 1.0).then_inc(s_const, 1)
            pool.memset(ident[:, :], 0.0).then_inc(s_const, 1)
            pool.memset(scan_keep[:, :, :], 1.0).then_inc(s_const, 1)
            pool.iota(iota_i[:, :], pattern=[[1, P]], base=0, channel_multiplier=0,
                      allow_small_or_imprecise_dtypes=True).then_inc(s_const, 1)
            pool.iota(tokp1[:, :], pattern=[[P, BLOCKS]], base=1, channel_multiplier=1,
                      allow_small_or_imprecise_dtypes=True).then_inc(s_const, 1)
            pool.iota(dump_col[:, :], pattern=[[0, 1]], base=DUMP, channel_multiplier=1,
                      allow_small_or_imprecise_dtypes=True).then_inc(s_const, 1)
            pool.iota(trash_col[:, :], pattern=[[0, 1]], base=TRASH, channel_multiplier=1,
                      allow_small_or_imprecise_dtypes=True).then_inc(s_const, 1)
            pool.iota(dump_before[:, :], pattern=[[0, P]], base=DUMP, channel_multiplier=1,
                      allow_small_or_imprecise_dtypes=True).then_inc(s_const, 1)
            pool.wait_ge(s_const, 9)
            pool.affine_select(out=ident[:, :], in_=ident[:, :], compare_op=ALU.not_equal, fill=1.0, base=0,
                               pattern=[[-1, P]], channel_multiplier=1).then_inc(s_const, 1)
            pool.affine_select(out=before[:, :], in_=ones[:, :], compare_op=ALU.is_gt, fill=0.0, base=0,
                               pattern=[[1, P]], channel_multiplier=-1).then_inc(s_const, 1)
            pool.affine_select(out=dump_before[:, :], in_=dump_before[:, :], compare_op=ALU.is_gt, fill=0.0, base=0,
                               pattern=[[-1, P]], channel_multiplier=1).then_inc(s_const, 1)
            pool.memset(scan_keep[:, :, 0:1], 0.0).then_inc(s_const, 1)

            tail = (ACCROWS - N) * D // P
            flat_x = x.rearrange("r d -> (r d)").rearrange("(q p f) -> q p f", p=P, q=PIECES - 1)
            flat_0 = acc[0][0:N, :].rearrange("r d -> (r d)").rearrange("(q p f) -> q p f", p=P, q=PIECES - 1)
            for n in range(PIECES):
                for a in range(CHAINS):
                    count = n * CHAINS + a
                    if 0 < count * PACE <= SB:
                        pool.wait_ge(s_xt, count * PACE)
                    if a:
                        rows = acc[a][n * ACCROWS // PIECES:(n + 1) * ACCROWS // PIECES, :]
                        pool.dma_start(rows.rearrange("(p q r) d -> p q (r d)", p=P, r=3),
                                       zero[:, :].rearrange("p (a f) -> p a f", a=1)
                                       .to_broadcast([P, ACCR // PIECES // 3, 3 * D])).then_inc(s_chain[a], 16)
                    elif n < PIECES - 1:
                        pool.dma_start(flat_0[n, :, :], flat_x[n, :, :]).then_inc(s_chain[0], 16)
                    else:
                        pool.dma_start(acc[0][N:ACCROWS, :].rearrange("r d -> (r d)").rearrange("(p f) -> p f", p=P),
                                       zero[:, 0:tail]).then_inc(s_chain[0], 16)
                    if count == SPLIT * 2 * GB // PACE - 1:
                        pool.wait_ge(s_late, 1)
                        pool.partition_all_reduce(late[:, 1:2], late[:, 0:1], P, bass.bass_isa.ReduceOp.add)\
                            .then_inc(s_latesum, 1)

            def add_rows(a, col, rows, done):
                pool.sem_inc(s_taken, 1)
                pool.indirect_dma_start(out=acc[a], out_offset=bass.IndirectOffsetOnAxis(ap=col, axis=0),
                                        in_=rows, in_offset=None, compute_op=ALU.add).then_inc(done, 16)

            pool.wait_ge(s_tables, 1)
            is_local = pool.value_load(flag_i[0:1, 0:1], min_val=0, max_val=1)
            with pool.If(is_local > 0):
                def scatter(it):
                    for k in range(U):
                        s = it * U + k
                        pool.wait_ge(s_msg, s + 1)
                        pool.wait_ge(s_idx, s + 1)
                        pool.wait_ge(s_chain[k % CHAINS], (it * (U // CHAINS) + k // CHAINS + PIECES) * 16)
                        add_rows(k % CHAINS, idxr[:, k % 8:k % 8 + 1], msg[:, k % 8, :], s_chain[k % CHAINS])
                turns(pool, ITER, scatter)
                for a in range(CHAINS):
                    pool.wait_ge(s_chain[a], 16 * (PIECES + STEPS // CHAINS))
                pool.nop().then_inc(s_graph, 1)
            with pool.Else():
                pool.wait_ge(s_S, SB)
                for a in range(CHAINS):
                    pool.wait_ge(s_chain[a], 16 * PIECES)
                pool.dma_start(support_dram.rearrange("(j p) d -> p j d", p=STRIDE), S[0:STRIDE, :, :]).then_inc(u_sup, 16)
                pool.wait_ge(u_sup, 16)
                pool.nop().then_inc(u_turn, 1)
                with pool.Fori(0, STEPS) as s:
                    pool.wait_ge(u_col, s + 1)
                    pool.sem_inc(s_taken, 1)
                    pool.indirect_dma_start(out=msg[:, 1, :], out_offset=None, in_=support_dram,
                                            in_offset=bass.IndirectOffsetOnAxis(ap=idxd[:, 0:1], axis=0))\
                        .then_inc(u_rows, 16)
                    pool.wait_ge(u_msg, s + 1)
                    add_rows(0, idxr[:, 0:1], msg[:, 0, :], u_sent)
                    pool.wait_ge(u_sent, s * 16 + 16)
                    pool.sem_inc(u_turn, 1)
                pool.nop().then_inc(s_graph, 1)

            def weights_low(e, c, h):
                if c == 0:
                    pool.wait_ge(s_whi, e + 1)
                    pool.sem_inc(s_taken, 1)
                if c < WCH // 2:
                    parts, whole, size = w1p[h].rearrange("p n k f -> p n (k f)"), w1s.rearrange("p k f -> p (k f)"), KD * F
                else:
                    parts, whole, size = w2p[h].rearrange("p n k d -> p n (k d)"), w2s.rearrange("p k d -> p (k d)"), KF * D
                size //= WCH // 2
                at = c % (WCH // 2) * size
                pool.tensor_tensor(out=parts[:, 1, at:at + size], in0=whole[:, at:at + size],
                                   in1=parts[:, 0, at:at + size].bitcast(f32), op=ALU.subtract).then_inc(s_wlo, 1)

            for w in range(GROUPS + 6):
                for stage in range(CHAINS, 0, -1):
                    q = w - stage
                    if not 0 <= q < GROUPS:
                        continue
                    if stage == 1:
                        pool.wait_ge(s_ld[q % 4], 16 * (q // 4 + 1))
                    else:
                        pool.wait_ge(s_sum[q % 4], 16 * ((CHAINS - 1) * (q // 4) + stage - 1))
                    if stage == CHAINS:
                        pool.nop().then_inc(s_xr, 1)
                        continue
                    pool.dma_start(xr[:, q * GB:(q + 1) * GB, 0:D],
                                   acc[stage][q * GB * P:(q + 1) * GB * P, :].rearrange("(j p) d -> p j d", p=P),
                                   accum_op=ALU.add).then_inc(s_sum[q % 4], 16)
                if 6 <= w < 6 + WCH:
                    weights_low(0, w - 6, 0)
                q = w - 6
                if q < 0:
                    continue
                if q == 0:
                    pool.wait_ge(s_bufz, 16 * BUF_PARTS)
                pool.wait_ge(r_slot, q + 1)
                for j in range(q * GB, (q + 1) * GB):
                    pool.indirect_dma_start(out=buf, out_offset=bass.IndirectOffsetOnAxis(ap=slots[:, j:j + 1], axis=0),
                                            in_=xr[:, j, :], in_offset=None, bounds_check=TRASH - 1,
                                            oob_is_err=False).then_inc(s_disp, 16)
            pool.wait_ge(s_disp, 16 * BLOCKS)
            pool.wait_ge(s_base, 16 * (GROUPS + 1))
            pool.nop().then_inc(s_routed, 1)
            pool.memset(res[:, :, :], 0.0).then_inc(s_resz, 1)

            pool.wait_ge(s_resz, 1)

            def send(pair):
                for q in range(2 * QUADS):
                    n = pair * (2 * QUADS) + q
                    for i in range(QT):
                        if i % 2 == 0:
                            pool.wait_ge(f_res, n * QT + i + 2)
                            pool.sem_inc(s_taken, 1)
                        pool.indirect_dma_start(out=out, out_offset=bass.IndirectOffsetOnAxis(ap=fidx[:, q % QUADS, i:i + 1], axis=0),
                                                in_=res[:, (q % 2) * QT + i, :], in_offset=None,
                                                bounds_check=N - 1, oob_is_err=False).then_inc(s_out[q % QUADS], 16)
                    if q % QUADS == 0 and not (isinstance(pair, int) and pair == NE // 2 - 1 and q):
                        for c in range(WCH):
                            weights_low(pair * 2 + q // QUADS + 1, c, 1 - q // QUADS)
            turns(pool, NE // 2, send)
            for q in range(QUADS):
                pool.wait_ge(s_out[q], 16 * NE * QT)

        @block.vector
        def _(dve):
            chain = [0]

            def link(ins):
                chain[0] += 1
                ins.then_inc(v_step, 1)
                dve.wait_ge(v_step, chain[0])

            srcI, dstI = (a.bitcast(i32) for a in (srcR, dstR))
            def norm_stats(rows, h, var_ready):
                for j in range(GB):
                    nc.vector.bn_stats(stats[:, h, j, :], rows(j))
                dve.drain()
                for j in range(GB):
                    nc.vector.bn_aggr(mv[:, h, j, :], stats[:, h, j, :])
                dve.drain()
                nc.vector.tensor_scalar(ve[:, h, :], mv[:, h, :, 1], EPS, None, ALU.add).then_inc(var_ready, 1)

            def norm_x(it):
                for h in range(2):
                    dve.wait_ge(s_xin[h], it * 32 + 32)
                    if isinstance(it, int) and 2 * it + h == SG - 1:
                        dve.wait_ge(s_xtail, 48)
                    norm_stats(lambda j: xin[:, h * GB + j, :], h, s_var)
                    dve.wait_ge(s_sd, it * 2 + h + 1)
                    nc.vector.reciprocal(rs[:, h, :], sd[:, h, :])
                    dve.drain()
                    for j in range(GB):
                        nc.vector.tensor_scalar(xin[:, h * GB + j, :], xin[:, h * GB + j, :], mv[:, h, j, 0:1],
                                                rs[:, h, j:j + 1], ALU.subtract, ALU.mult).then_inc(s_xn, 1)
            def edge_tables():
                dve.wait_ge(s_const, 13)
                for i in range(3):
                    dve.wait_ge(s_edge[i], 48)
                nc.vector.tensor_scalar(valid[:, :], tokp1[:, :], float(N), None, ALU.is_le)
                link(nc.vector.tensor_scalar(hi_i[:, 0, :], dstI[:, :, 0], 4, None, ALU.arith_shift_right))
                link(nc.vector.tensor_scalar(hi_i[:, 1, :], hi_i[:, 0, :], float(DIV), None, ALU.mult))
                link(nc.vector.tensor_scalar(hi_i[:, 0, :], hi_i[:, 1, :], 16, None, ALU.arith_shift_right))
                link(nc.vector.tensor_copy(keys[:, 0, :], hi_i[:, 0, :]))
                nc.vector.tensor_scalar(keys[:, 1, :], keys[:, 0, :], float(STRIDE), None, ALU.mult)
                nc.vector.tensor_copy(srcR[:, :, :], srcI[:, :, :])
                link(nc.vector.tensor_copy(dstR[:, :, :], dstI[:, :, :]))
                first = keys[:, 1, :].rearrange("p (c a) -> p c a", a=1).to_broadcast([P, TC, P])
                link(nc.vector.tensor_tensor(rel[:, :, :], dstR[:, :, :], first, ALU.subtract))
                link(nc.vector.tensor_scalar(outside[:, :, :], rel[:, :, :], 0.0, None, ALU.is_lt))
                link(nc.vector.scalar_tensor_tensor(outside[:, :, :], rel[:, :, :], float(P - 1), outside[:, :, :],
                                                    ALU.is_gt, ALU.add))
                nc.vector.tensor_reduce(late[:, 0:1], outside[:, :, :], AX.XY, ALU.add).then_inc(s_late, 1)
                dve.wait_ge(s_latesum, 1)
                link(nc.vector.tensor_scalar(flag_f[:, :], late[:, 1:2], 0.0, None, ALU.is_equal))
                nc.vector.tensor_copy(flag_i[:, :], flag_f[:, :])
                link(nc.vector.tensor_scalar(keys[:, :, :], keys[:, :, :], flag_f[:, 0:1], None, ALU.mult))
                nc.vector.tensor_tensor(dstR[:, :, :], dstR[:, :, :], first, ALU.subtract).then_inc(s_tiles, 1)

            norm_x(0)
            with dve.Fori(1, SPLIT) as it:
                norm_x(it)
            edge_tables()
            with dve.Fori(SPLIT, SG // 2 - 1) as it:
                norm_x(it)
            norm_x(SG // 2 - 1)

            for c in range(TC):
                dve.wait_ge(s_sel, c + 1)
                bank = ps[:, 1 + c % 2, :]
                n = min(P, STEPS - c * P)
                nc.vector.tensor_copy(btab[0:1, c * P:c * P + n], bank[0:1, 3 * P:3 * P + n])
                nc.vector.tensor_copy(cols[:, c * P:(c + 1) * P, :].rearrange("p e n -> p n e"),
                                      bank[:, 0:3 * P].rearrange("p (n e) -> p n e", n=3)).then_inc(s_selread, 1)
            dve.wait_ge(s_selread, TC)
            quad = btab[0:1, :].rearrange("a (n k) -> a n k", k=4)
            link(nc.vector.tensor_copy(bpack[0:1, :], quad[:, :, 0]))
            for k in range(1, 4):
                link(nc.vector.tensor_scalar(bpart[0:1, k % 2, :], quad[:, :, k], 7 * k, None, ALU.logical_shift_left))
                link(nc.vector.tensor_tensor(bpack[0:1, :], bpack[0:1, :], bpart[0:1, k % 2, :], ALU.bitwise_or))
            nc.vector.memset(ohx[:, :, 0:1], 0.0).then_inc(s_tables, 1)

            is_local = dve.value_load(flag_i[0:1, 0:1], min_val=0, max_val=1)
            with dve.If(is_local > 0):
                dve.wait_ge(s_S, SB)

                def take_cols(half, n):
                    nc.vector.tensor_copy(colring[:, half, :, :], cols[:, bass.ds(n * 8, 8), :]).then_inc(s_col, 1)

                take_cols(0, 0)

                def edges(it):
                    last = isinstance(it, int) and it == ITER - 1
                    for k in range(U):
                        s = it * U + k
                        half, c = k // 8, k % 8
                        if k == 4:
                            take_cols(1, it * 2 + 1)
                        if k == 12 and not last:
                            take_cols(0, it * 2 + 2)
                        if c == 0:
                            dve.wait_ge(s_col, it * 2 + half + 1)
                        src_c, dst_c, w_c = (colring[:, half, c, n:n + 1] for n in range(3))
                        dve.wait_ge(s_srow, s + 1)
                        row = ps[:, k % 4, 0:P]
                        nc.vector.scalar_tensor_tensor(junk[:, k % 2, :], row, src_c, dump_before[:, :],
                                                       ALU.is_equal, ALU.mult, accum_out=dups[:, c:c + 1])\
                            .then_inc(s_dup, 1)
                        since(dve, s_g, s - 3)
                        nc.vector.tensor_scalar(eqs[:, k % 4, :], row, src_c, None, ALU.is_equal).then_inc(s_eq, 1)
                        nc.vector.tensor_scalar(ohw[:, k % 4, :], iota_i[:, 0:P], dst_c, w_c, ALU.is_equal, ALU.mult)\
                            .then_inc(s_ohw, 1)
                        if not isinstance(s, int) or s >= 8:
                            dve.wait_ge(s_chain[k % CHAINS], (it * (U // CHAINS) + k // CHAINS + PIECES - 1) * 16)
                        dve.wait_ge(s_dup, s + 1)
                        nc.vector.tensor_scalar(idxr[:, c:c + 1], dups[:, c:c + 1], src_c, dump_col[:, 0:1],
                                                ALU.max, ALU.min).then_inc(s_idx, 1)
                turns(dve, ITER, edges)
            with dve.Else():
                dve.wait_ge(s_S, SB)
                with dve.Fori(0, STEPS) as s:
                    dve.wait_ge(u_turn, s + 1)
                    nc.vector.tensor_copy(idxd[:, 0:1], cols[:, bass.ds(s, 1), 1])
                    nc.vector.tensor_copy(colring[:, 0, 0:1, :], cols[:, bass.ds(s, 1), :]).then_inc(u_col, 1)
                    dve.wait_ge(u_srow, s + 1)
                    nc.vector.scalar_tensor_tensor(junk[:, 0, :], ps[:, 0, 0:P], colring[:, 0, 0, 0:1], dump_before[:, :],
                                                   ALU.is_equal, ALU.mult, accum_out=dups[:, 0:1]).then_inc(u_dup, 1)
                    nc.vector.tensor_scalar(eqs[:, 0, :], ps[:, 0, 0:P], colring[:, 0, 0, 0:1], colring[:, 0, 0, 2:3],
                                            ALU.is_equal, ALU.mult)
                    dve.wait_ge(u_dup, s + 1)
                    nc.vector.tensor_scalar(idxr[:, 0:1], dups[:, 0:1], colring[:, 0, 0, 0:1], dump_col[:, 0:1],
                                            ALU.max, ALU.min).then_inc(u_idx, 1)
                dve.nop()

            dve.wait_ge(s_graph, 1)
            dve.wait_ge(s_gate, 48)

            def stats_group(q, h):
                dve.wait_ge(s_xr, q + 1)
                norm_stats(lambda j: xr[:, bass.ds(q * GB + j, 1), 0:D].rearrange("p a d -> p (a d)"), h, r_var)

            def scale_group(q, h):
                dve.wait_ge(r_sd, q + 1)
                group = lambda c: xr[:, bass.ds(q * GB, GB), c]
                nc.vector.reciprocal(rs[:, h, :], sd[:, h, :])
                dve.drain()
                nc.vector.tensor_copy(group(RSTD), rs[:, h, :])
                nc.vector.scalar_tensor_tensor(small[:, 0, :], mv[:, h, :, 0], -1.0, rs[:, h, :], ALU.mult, ALU.mult)
                dve.drain()
                nc.vector.tensor_copy(group(NMR), small[:, 0, :])
                nc.vector.tensor_copy(group(TOK), tokp1[:, bass.ds(q * GB, GB)]).then_inc(r_rs, 1)

            for q in range(2):
                stats_group(q, q)
                scale_group(q, q)

            def weights_high(e, h):
                dve.wait_ge(s_ew, e * 48 + 48)
                nc.vector.tensor_copy(w1p[h][:, 0, :, :], w1s[:, :, :])
                nc.vector.tensor_copy(w2p[h][:, 0, :, :], w2s[:, :, :]).then_inc(s_whi, 1)

            def route(it):
                for h in range(2):
                    q = it * 2 + h
                    if isinstance(it, int) and q == 1:
                        weights_high(0, 0)
                    ahead = not (isinstance(it, int) and q >= LASTG - 1)
                    group = lambda c: xr[:, bass.ds(q * GB, GB), c]
                    wide = lambda a: a.rearrange("p (j a) -> p j a", a=1).to_broadcast([P, GB, NE])
                    over_j = lambda a: a.rearrange("p (a e) -> p a e", a=1).to_broadcast([P, GB, NE])
                    dve.wait_ge(r_lg, (q + 1) * GB)
                    logit = ps[:, 6 + h, 0:GB * NE].rearrange("p (j e) -> p j e", e=NE)
                    nc.vector.tensor_tensor(lg[:, h, :, :], logit, over_j(gbs[:, :]), ALU.add)
                    dve.drain()
                    nc.vector.tensor_reduce(small[:, 1, :], lg[:, h, :, :], AX.X, ALU.max)
                    dve.drain()
                    nc.vector.tensor_tensor(lg[:, h, :, :], lg[:, h, :, :], wide(small[:, 1, :]), ALU.subtract)\
                        .then_inc(r_l, 1)
                    dve.wait_ge(r_ex, q + 1)
                    nc.vector.tensor_reduce(small[:, 2, :], lg[:, h, :, :], AX.X, ALU.add)
                    dve.drain()
                    nc.vector.reciprocal(small[:, 3, :], small[:, 2, :])
                    dve.drain()
                    nc.vector.tensor_tensor(pr[:, h, :, :], lg[:, h, :, :], wide(small[:, 3, :]), ALU.mult)
                    dve.drain()
                    nc.vector.tensor_reduce(small[:, 4, :], pr[:, h, :, :], AX.X, ALU.max)
                    dve.drain()
                    nc.vector.tensor_copy(group(PRB), small[:, 4, :])
                    nc.vector.tensor_tensor(cand[:, :, :], pr[:, h, :, :], wide(small[:, 4, :]), ALU.is_equal)
                    dve.drain()
                    nc.vector.scalar_tensor_tensor(cand[:, :, :], cand[:, :, :], float(-NE), over_j(iota_i[:, 0:NE]),
                                                   ALU.mult, ALU.add)
                    dve.drain()
                    nc.vector.tensor_reduce(small[:, 5, :], cand[:, :, :], AX.X, ALU.min)
                    dve.drain()
                    nc.vector.tensor_tensor(cand[:, :, :], cand[:, :, :], wide(small[:, 5, :]), ALU.is_equal)
                    dve.drain()
                    chosen = ohx[:, :, 1:GB + 1].rearrange("p e j -> p j e")
                    nc.vector.tensor_tensor(chosen, cand[:, :, :], wide(valid[:, bass.ds(q * GB, GB)]), ALU.mult)
                    dve.drain()
                    nc.vector.tensor_tensor_scan(cum[:, :, :].rearrange("p e j -> p (e j)"),
                                                 scan_keep[:, :, :].rearrange("p e j -> p (e j)"),
                                                 ohx[:, :, :].rearrange("p e j -> p (e j)"), 0.0, ALU.mult, ALU.add)\
                        .then_inc(r_cum, 1)
                    if ahead:
                        stats_group(q + 2, h)
                    dve.wait_ge(r_pos, q + 1)
                    count = ps[:, 5, 0:NE * GB].rearrange("p (e j) -> p j e", e=NE)
                    nc.vector.tensor_tensor(pos[:, :, :], count, chosen, ALU.mult)
                    nc.vector.tensor_scalar(small[:, 5, :], small[:, 5, :], float(NE), float(SLOTS), ALU.add, ALU.mult)
                    dve.drain()
                    nc.vector.tensor_reduce(small[:, 6, :], pos[:, :, :], AX.X, ALU.add)
                    nc.vector.tensor_copy(ohx[:, :, 0:1], cum[:, :, GB:GB + 1])
                    dve.drain()
                    nc.vector.scalar_tensor_tensor(small[:, 7, :], small[:, 6, :], float(CAP), valid[:, bass.ds(q * GB, GB)],
                                                   ALU.is_lt, ALU.mult)
                    nc.vector.scalar_tensor_tensor(small[:, 6, :], small[:, 6, :], trash_col[:, 0:1], small[:, 5, :],
                                                   ALU.subtract, ALU.add)
                    dve.drain()
                    nc.vector.tensor_tensor(small[:, 6, :], small[:, 6, :], small[:, 7, :], ALU.mult)
                    dve.drain()
                    nc.vector.tensor_scalar(slots[:, bass.ds(q * GB, GB)], small[:, 6, :], trash_col[:, 0:1], None, ALU.add)\
                        .then_inc(r_slot, 1)
                    if ahead:
                        scale_group(q + 2, h)
            turns(dve, GROUPS // 2, route)

            first = live_bit[:, :, 0]
            nc.vector.tensor_scalar(first, iota_i[0:1, 0:QUADS], float(QT * P), None, ALU.mult)
            for q in range(QUADS):
                nc.vector.memset(live_bit[:, q:q + 1, 1], float(1 << q))
            dve.wait_ge(s_total, 1)
            dve.drain()
            nc.vector.tensor_tensor(live[:, :, :], ps[0:1, 5, 0:NE].rearrange("a (e q) -> a e q", q=1).to_broadcast([1, NE, QUADS]),
                                    live_bit[:, :, 0:1].rearrange("a q k -> a k q").to_broadcast([1, NE, QUADS]), ALU.is_gt)
            dve.drain()
            nc.vector.tensor_tensor(live[:, :, :], live[:, :, :],
                                    live_bit[:, :, 1:2].rearrange("a q k -> a k q").to_broadcast([1, NE, QUADS]), ALU.mult)
            dve.drain()
            nc.vector.tensor_reduce(live_sum[:, :], live[:, :, :], AX.X, ALU.add)
            dve.drain()
            nc.vector.scalar_tensor_tensor(live_pack[:, :], live_sum[:, 1:NE:2], float(1 << QUADS), live_sum[:, 0:NE:2],
                                           ALU.mult, ALU.add).then_inc(s_live, 1)

            dve.wait_ge(s_routed, 1)
            dve.wait_ge(s_live, 1)
            dve.wait_ge(s_resz, 1)

            def take_xT(n):
                dve.wait_ge(f_xt, n + 1)
                nc.vector.tensor_copy(fxT[:, 0, :, :], ps[:, 3:3 + KD, :])
                dve.drain()
                nc.vector.tensor_tensor(fxT[:, 1, :, :], ps[:, 3:3 + KD, :], fxT[:, 0, :, :].bitcast(f32),
                                        ALU.subtract).then_inc(f_xts, 1)

            take_xT(0)

            def finish(pair):
                last = isinstance(pair, int) and pair == NE // 2 - 1
                holds = dve.value_load(live_pack[0:1, bass.ds(pair, 1)], min_val=0, max_val=(1 << 2 * QUADS) - 1)
                for q in range(2 * QUADS):
                    n = pair * (2 * QUADS) + q
                    within, h = q % QUADS, q % 2
                    slot = q // QUADS * 2 + h

                    def taken():
                        since(dve, s_out[within], (pair * 2 + q // QUADS) * (16 * QT))
                        tok = fin_rows[:, slot * QT:(slot + 1) * QT, TOK]
                        nc.vector.tensor_scalar(fsm[:, :], tok, 0.0, float(2 * N), ALU.is_equal, ALU.mult)
                        dve.drain()
                        nc.vector.scalar_tensor_tensor(fidx[:, within, :], tok, -1.0, fsm[:, :], ALU.add, ALU.add)
                        for f in range(KF):
                            dve.wait_ge(f_hs, n * KF + f + 1)
                            nc.vector.tensor_tensor(hT[:, 1, f, :], h32[:, f % 4, :], hT[:, 0, f, :].bitcast(f32),
                                                    ALU.subtract).then_inc(f_hl, 1)
                        holding(dve, holds, pair, q, lambda m, e, k: take_xT(m), lambda c: dve.drain().then_inc(f_xts, c))
                        since(dve, s_out[(within + 2) % QUADS], (pair * 2 + (q + 2) // QUADS) * (16 * QT))
                        for i in range(0, QT, 2):
                            rows = fin_rows[:, slot * QT + i:slot * QT + i + 2, :]
                            t, large, r = guard[:, 0, :, :], guard[:, 1, :, :], guard[:, 2, :, :]
                            dve.wait_ge(f_y, n * QT + i + 2)
                            nc.vector.tensor_tensor(t, ps[:, 5 + i // 2, :].rearrange("p (i d) -> p i d", i=2),
                                                    b2s[:, q // QUADS:q // QUADS + 1, :].to_broadcast([P, 2, D]),
                                                    ALU.add).then_inc(f_yread, 1)
                            dve.drain()
                            nc.vector.tensor_tensor(t, t, rows[:, :, PRB:PRB + 1].to_broadcast([P, 2, D]), ALU.mult)
                            dve.drain()
                            nc.vector.tensor_scalar(masks[:, :, :], t, 0.0, 0.0, ALU.mult, ALU.is_equal)
                            nc.vector.tensor_scalar(large, t, FLT_MAX, 1e4, ALU.is_gt, ALU.mult)
                            nc.vector.tensor_scalar(r, t, -FLT_MAX, -1e4, ALU.is_lt, ALU.mult)
                            dve.drain()
                            nc.vector.tensor_tensor(r, r, large, ALU.add)
                            dve.drain()
                            nc.vector.copy_predicated(r, masks[:, :, :], t)
                            dve.drain()
                            nc.vector.tensor_tensor(res[:, h * QT + i:h * QT + i + 2, :], r, rows[:, :, 0:D],
                                                    ALU.add).then_inc(f_res, 2)

                    if within == 0:
                        taken()
                        if not (last and q):
                            weights_high(pair * 2 + q // QUADS + 1, 1 - q // QUADS)
                        continue
                    with dve.If(((holds >> q) & 1) > 0):
                        taken()
                    with dve.Else():
                        since(dve, s_out[within], (pair * 2 + q // QUADS) * (16 * QT))
                        nc.vector.memset(fidx[:, within, :], 2 * N)
                        dve.drain().then_inc(f_hl, KF)
                        dve.drain().then_inc(f_yread, QT // 2)
                        dve.drain().then_inc(f_res, QT)
            turns(dve, NE // 2, finish)

        @block.scalar
        def _(act):
            def root(g, h, var_ready, done):
                act.wait_ge(var_ready, g + 1)
                nc.scalar.activation(sd[:, h, :], ve[:, h, :], ACT.Sqrt).then_inc(done, 1)

            root(0, 0, s_var, s_sd)

            def take_xT(n, r):
                act.wait_ge(s_xt, n + 1)
                since(act, s_sp, n - 1)
                nc.scalar.activation(xTs[:, r * KD:(r + 1) * KD, :],
                                     ps[:, 4 + r, 0:D].rearrange("p (k n) -> p k n", k=KD), ACT.Copy).then_inc(s_xts, 1)

            take_xT(0, 0)

            def support(it):
                for h in range(2):
                    for j in range(GB):
                        last = isinstance(it, int) and it * 2 + h == SG - 1
                        if j == 2 and not last:
                            root(it * 2 + h + 1, 1 - h, s_var, s_sd)
                        n = (it * 2 + h) * GB + j
                        r = (h * GB + j) % 2
                        if not (last and j == GB - 1):
                            take_xT(n + 1, 1 - r)
                        act.wait_ge(s_sp, n + 1)
                        act.sem_inc(a_taken, 1)
                        nc.scalar.activation(S[:, bass.ds(n, 1), :].rearrange("p a d -> p (a d)"), ps[:, 6 + r, 0:D], ACT.Copy)\
                            .then_inc(s_S, 1)
            turns(act, SG // 2, support)

            act.wait_ge(s_tables, 1)
            is_local = act.value_load(flag_i[0:1, 0:1], min_val=0, max_val=1)
            with act.If(is_local > 0):
                def take_g(s, r):
                    act.wait_ge(s_g, s + 1)
                    since(act, s_m, s - 3)
                    nc.scalar.activation(gsb[:, r, :], ps[:, 4 + r % 2, 0:P], ACT.Copy)\
                        .then_inc(s_gs, 1)

                take_g(0, 0)

                def rows(it):
                    last = isinstance(it, int) and it == ITER - 1
                    for k in range(U):
                        s = it * U + k
                        if not (last and k == U - 1):
                            take_g(s + 1, (k + 1) % 4)
                        act.wait_ge(s_m, s + 1)
                        if not isinstance(s, int) or s >= 8:
                            act.wait_ge(s_chain[k % CHAINS], (it * (U // CHAINS) + k // CHAINS + PIECES - 1) * 16)
                        nc.scalar.activation(msg[:, k % 8, :], ps[:, 6 + k % 2, 0:D], ACT.Copy).then_inc(s_msg, 1)
                turns(act, ITER, rows)
            with act.Else():
                with act.Fori(0, STEPS) as s:
                    act.wait_ge(u_m, s + 1)
                    nc.scalar.activation(msg[:, 0, :], ps[:, 4, 0:D], ACT.Copy).then_inc(u_msg, 1)
                act.nop()

            def exponents(q, h):
                act.wait_ge(r_l, q + 1)
                nc.scalar.activation(lg[:, h, :, :], lg[:, h, :, :], ACT.Exp).then_inc(r_ex, 1)

            root(0, 0, r_var, r_sd)

            def route(it):
                for h in range(2):
                    q = it * 2 + h
                    act.wait_ge(r_rs, q + 1)

                    def norm(j):
                        n = q * GB + j
                        r = (h * GB + j) % 2
                        since(act, r_xt, n - 1)
                        if not (isinstance(n, int) and n < 2):
                            act.sem_inc(a_taken, 1)
                        row = lambda lo, hi: xr[:, bass.ds(n, 1), lo:hi].rearrange("p a d -> p (a d)")
                        nc.scalar.activation(rxn[:, r, :], row(0, D), ACT.Identity, bias=row(NMR, NMR + 1),
                                             scale=row(RSTD, RSTD + 1)).then_inc(r_xn, 1)

                    norm(0)
                    for j in range(GB):
                        n = q * GB + j
                        r = (h * GB + j) % 2
                        if j + 1 < GB:
                            norm(j + 1)
                        if j == 1 and not (isinstance(q, int) and q == 0):
                            exponents(q - 1, 1 - h)
                        if j == GB - 2 and not (isinstance(q, int) and q == LASTG):
                            root(q + 1, 1 - h, r_var, r_sd)
                        act.wait_ge(r_xt, n + 1)
                        since(act, r_lg, n - 1)
                        nc.scalar.activation(rxT[:, r * KD:(r + 1) * KD, :],
                                             ps[:, r, 0:D].rearrange("p (k n) -> p k n", k=KD), ACT.Copy).then_inc(r_xts, 1)
            turns(act, GROUPS // 2, route)
            exponents(LASTG, LASTG % 2)

            act.wait_ge(s_routed, 1)
            act.wait_ge(s_live, 1)

            def norm_quad(pair, n, e, q):
                slot = e % 2 * 2 + q % 2
                act.wait_ge(s_rows[slot], ((pair + e // 2) * 2 + q // 2) * 16 + 16)
                for i in range(QT):
                    row = fin_rows[:, slot * QT + i, :]
                    nc.scalar.activation(fxn[:, i, :], row[:, 0:D], ACT.Identity, bias=row[:, NMR:NMR + 1],
                                         scale=row[:, RSTD:RSTD + 1]).then_inc(f_xn, 1)

            norm_quad(0, 0, 0, 0)

            def hidden(pair):
                holds = act.value_load(live_pack[0:1, bass.ds(pair, 1)], min_val=0, max_val=(1 << 2 * QUADS) - 1)
                for q in range(2 * QUADS):
                    n = pair * (2 * QUADS) + q

                    def taken():
                        for f in range(KF):
                            act.wait_ge(f_h, n * KF + f + 1)
                            since(act, f_hl, n * KF + f - 3)
                            e = pair * 2 + q // QUADS
                            act.sem_inc(a_taken, 1)
                            nc.scalar.activation(h32[:, f % 4, :], ps[:, HB[f % 4], :], ACT.Relu,
                                                 bias=b1s[:, bass.ds(e, 1), f])
                            if f == 0:
                                since(act, f_y, n * QT)
                                act.sem_inc(a_taken, 1)
                            nc.scalar.activation(hT[:, 0, f, :], ps[:, HB[f % 4], :], ACT.Relu,
                                                 bias=b1s[:, bass.ds(e, 1), f]).then_inc(f_hs, 1)
                            if f == 3:
                                act.wait_ge(f_xt, n + 1)
                                holding(act, holds, pair, q, lambda m, e, k: norm_quad(pair, m, e, k),
                                        lambda c: act.drain().then_inc(f_xn, c * QT))

                    if q % QUADS == 0:
                        taken()
                        continue
                    with act.If(((holds >> q) & 1) > 0):
                        taken()
                    with act.Else():
                        act.drain().then_inc(f_hs, KF)
                        act.nop()
            turns(act, NE // 2, hidden)

        @block.tensor
        def _(pe):
            pe.wait_ge(s_const, 13)
            pe.wait_ge(s_w, 16)

            def x_transpose(it, p):
                n = it * (2 * GB) + p
                p %= 2 * GB
                pe.wait_ge(s_xn, n + 1)
                since(pe, s_xts, n - 1)
                for k in range(KD):
                    last = nc.tensor.transpose(ps[:, 4 + p % 2, k * P:(k + 1) * P], xin[:, p, k * P:(k + 1) * P], ident[:, :])
                last.then_inc(s_xt, 1)

            x_transpose(0, 0)

            def support(it):
                for p in range(2 * GB):
                    n = it * (2 * GB) + p
                    if not (isinstance(it, int) and n == SB - 1):
                        x_transpose(it, p + 1)
                    pe.wait_ge(s_xts, n + 1)
                    since(pe, s_S, n - 1)
                    for k in range(KD):
                        last = nc.tensor.matmul(ps[:, 6 + p % 2, 0:D], xTs[:, p % 2 * KD + k, :], Ws[:, k, :],
                                                start=k == 0, stop=k == KD - 1)
                    last.then_inc(s_sp, 1)
            turns(pe, SG // 2, support)

            pe.wait_ge(s_tiles, 1)
            for c in range(TC):
                since(pe, s_selread, c - 1)
                for n, table in enumerate((srcR, dstR, wR, None)):
                    rows = table[:, c, :] if table is not None else keys[:, 0, c:c + 1].to_broadcast([P, P])
                    last = nc.tensor.transpose(ps[:, 1 + c % 2, n * P:(n + 1) * P], rows, ident[:, :])
                last.then_inc(s_sel, 1)

            pe.wait_ge(s_tables, 1)
            pe.wait_ge(s_S, SB)
            is_local = pe.value_load(flag_i[0:1, 0:1], min_val=0, max_val=1)
            with pe.If(is_local > 0):
                def src_row(it, k):
                    s = it * U + k
                    half, c = k // 8 % 2, k % 8
                    if c == 0:
                        pe.wait_ge(s_col, it * 2 + k // 8 + 1)
                    since(pe, s_eq, s - 3)
                    nc.tensor.transpose(ps[:, k % 4, 0:P],
                                        colring[:, half, c, 0:1].to_broadcast([P, P]), ident[:, :]).then_inc(s_srow, 1)

                def g_of(s, r):
                    pe.wait_ge(s_ohw, s + 1)
                    since(pe, s_gs, s - 1)
                    nc.tensor.matmul(ps[:, 4 + r % 2, 0:P], ohw[:, r, :], eqs[:, r, :],
                                     start=True, stop=True).then_inc(s_g, 1)

                for k in range(3):
                    src_row(0, k)
                g_of(0, 0)

                def steps(it):
                    last = isinstance(it, int) and it == ITER - 1
                    for k in range(U):
                        s = it * U + k
                        if k % 4 == 0:
                            packed = pe.value_load(bpack[0:1, bass.ds(it * (U // 4) + k // 4, 1)], min_val=0,
                                                   max_val=(1 << 28) - 1)
                        if not (last and k + 3 >= U):
                            src_row(it, k + 3)
                        if not (last and k == U - 1):
                            g_of(s + 1, (k + 1) % 4)
                        b = nc.s_assert_within((packed >> (7 * (k % 4))) & 127, 0, SB - 1,
                                               skip_runtime_bounds_check_because="the block of a dst")
                        pe.wait_ge(s_gs, s + 1)
                        since(pe, s_msg, s - 1)
                        nc.tensor.matmul(ps[:, 6 + k % 2, 0:D], gsb[:, k % 4, :],
                                         S[:, bass.ds(b, 1), :].rearrange("p a d -> p (a d)"),
                                         start=True, stop=True).then_inc(s_m, 1)
                turns(pe, ITER, steps)
            with pe.Else():
                with pe.Fori(0, STEPS) as s:
                    pe.wait_ge(u_col, s + 1)
                    nc.tensor.transpose(ps[:, 0, 0:P], colring[:, 0, 0, 0:1].to_broadcast([P, P]), ident[:, :])\
                        .then_inc(u_srow, 1)
                    pe.wait_ge(u_idx, s + 1)
                    pe.wait_ge(u_rows, s * 16 + 16)
                    nc.tensor.matmul(ps[:, 4, 0:D], eqs[:, 0, :], msg[:, 1, :], start=True, stop=True).then_inc(u_m, 1)
                pe.nop()

            pe.wait_ge(s_gate, 48)
            pe.wait_ge(s_graph, 1)

            def positions(q):
                pe.wait_ge(r_cum, q + 1)
                count = ps[:, 5, 0:NE * GB].rearrange("p (e j) -> p e j", e=NE)
                nc.tensor.matmul(count, before[:, :], ohx[:, :, 1:GB + 1], start=True, stop=False)
                nc.tensor.matmul(count, ones[:, :], cum[:, :, 0:GB], start=False, stop=True).then_inc(r_pos, 1)

            def route(it):
                for h in range(2):
                    q = it * 2 + h

                    def transpose(j):
                        n = q * GB + j
                        r = (h * GB + j) % 2
                        pe.wait_ge(r_xn, n + 1)
                        since(pe, r_xts, n - 1)
                        for k in range(KD):
                            last = nc.tensor.transpose(ps[:, r, k * P:(k + 1) * P], rxn[:, r, k * P:(k + 1) * P], ident[:, :])
                        last.then_inc(r_xt, 1)

                    transpose(0)
                    for j in range(GB):
                        n = q * GB + j
                        r = (h * GB + j) % 2
                        if j + 1 < GB:
                            transpose(j + 1)
                        pe.wait_ge(r_xts, n + 1)
                        if j == 0:
                            since(pe, r_l, q - 1)
                        if j == GB - 3 and not (isinstance(q, int) and q == 0):
                            positions(q - 1)
                        for k in range(KD):
                            last = nc.tensor.matmul(ps[:, 6 + h, j * NE:(j + 1) * NE], rxT[:, r * KD + k, :], gws[:, k, :],
                                                    start=k == 0, stop=k == KD - 1)
                        last.then_inc(r_lg, 1)
            turns(pe, GROUPS // 2, route)
            positions(LASTG)
            pe.wait_ge(r_slot, GROUPS)
            nc.tensor.matmul(ps[:, 5, 0:NE], ones[:, :], cum[:, :, GB], start=True, stop=True).then_inc(s_total, 1)

            pe.wait_ge(s_live, 1)

            def quad_T(n):
                for i in range(QT):
                    pe.wait_ge(f_xn, n * QT + i + 1)
                    for k in range(KD):
                        last = nc.tensor.transpose(ps[:, 3 + k, i * P:(i + 1) * P], fxn[:, i, k * P:(k + 1) * P], ident[:, :])
                last.then_inc(f_xt, 1)

            quad_T(0)

            def layers(pair):
                holds = pe.value_load(live_pack[0:1, bass.ds(pair, 1)], min_val=0, max_val=(1 << 2 * QUADS) - 1)
                for q in range(2 * QUADS):
                    n = pair * (2 * QUADS) + q
                    e = q // QUADS

                    def taken():
                        pe.wait_ge(f_xts, n + 1)
                        if q % QUADS == 0:
                            pe.wait_ge(s_wlo, pair * (2 * WCH) + (e + 1) * WCH)
                        for f in range(KF):
                            since(pe, f_hs, n * KF + f - 3)
                            for k in range(KD):
                                for a, b in PASSES:
                                    last = nc.tensor.matmul(ps[:, HB[f % 4], :], w1p[e][:, a, k, f * P:(f + 1) * P],
                                                            fxT[:, b, k, :], start=k == 0 and a + b == 0,
                                                            stop=k == KD - 1 and (a, b) == PASSES[-1])
                            last.then_inc(f_h, 1)
                        holding(pe, holds, pair, q, lambda m, e, k: quad_T(m), lambda c: pe.drain().then_inc(f_xt, c))
                        for i in range(QT):
                            if i % 2 == 0:
                                since(pe, f_yread, n * (QT // 2) + i // 2 - 1)
                            for f in range(KF):
                                if i == 0:
                                    pe.wait_ge(f_hl, n * KF + f + 1)
                                for a, b in PASSES:
                                    last = nc.tensor.matmul(ps[:, 5 + i // 2, i % 2 * D:(i % 2 + 1) * D],
                                                            hT[:, a, f, i * P:(i + 1) * P], w2p[e][:, b, f, :],
                                                            start=f == 0 and a + b == 0,
                                                            stop=f == KF - 1 and (a, b) == PASSES[-1])
                            last.then_inc(f_y, 1)

                    if q % QUADS == 0:
                        taken()
                        continue
                    with pe.If(((holds >> q) & 1) > 0):
                        taken()
                    with pe.Else():
                        pe.drain().then_inc(f_h, KF)
                        pe.drain().then_inc(f_y, QT)
            turns(pe, NE // 2, layers)


_INS = ['x', 'src', 'dst', 'edge_weight', 'L0_gnn_W', 'L0_ffn_gate_w', 'L0_ffn_gate_b', 'L0_ffn_w1', 'L0_ffn_b1',
        'L0_ffn_w2', 'L0_ffn_b2']


def kernel(**inputs):
    import numpy as _np
    import concourse.bacc as _bacc
    from concourse import mybir as _mybir
    from concourse.bass_utils import run_bass_kernel_spmd as _run

    nc = _bacc.Bacc("TRN2", target_bir_lowering=False, num_devices=1)
    arrays, args = {}, []
    for name in _INS:
        a = _np.ascontiguousarray(inputs[name])
        arrays[f"in_{name}_dram"] = a
        args.append(nc.dram_tensor(f"in_{name}_dram", a.shape, _mybir.dt.from_np(a.dtype), kind="ExternalInput").ap())
    shape = inputs["x"].shape
    args.append(nc.dram_tensor("out_0_dram", shape, _mybir.dt.float32, kind="ExternalOutput").ap())
    bass_gnn_then_top1_ffn(nc, *args)
    r = _run(nc, [arrays], core_ids=[0])
    return r.results[0]["out_0_dram"]
```
